# Optimizing a Trainium2 kernel written in Bass

```python
import numpy as np
import jax
import jax.numpy as jnp

def _softmax(x, axis=-1):
    return jax.nn.softmax(x, axis=axis)

def _gelu(x):
    return jax.nn.gelu(x, approximate=True)

def _silu(x):
    return jax.nn.silu(x)

def _sigmoid(x):
    return jax.nn.sigmoid(x)

def _layernorm(x, axis=-1, eps=1e-05):
    m = jnp.mean(x, axis=axis, keepdims=True)
    v = jnp.var(x, axis=axis, keepdims=True)
    return (x - m) / jnp.sqrt(v + eps)

def _scatter_add(tgt, idx, src, axis=0):
    return tgt.at[idx].add(src)

def _segment_sum(src, seg, n):
    return jax.ops.segment_sum(src, seg, n)
kernel_name = 'mk_flamingo_gated_d1_seqx_r4_2f8323'

def setup_inputs(seed: int=0):
    np.random.seed(seed)
    _w = jnp.asarray

    def _rec_inputs():
        import jax
        import jax.numpy as jnp
        _rk = jax.random.key(seed)
        x = -7.109e-05 + 0.9999 * jax.random.normal(jax.random.fold_in(_rk, 1), (16, 128, 1024), jnp.float32)
        _lenS = 128 - jax.random.randint(jax.random.fold_in(_rk, 7), (16,), 0, max(1, 128 // 4) + 1, jnp.int32)
        _lenS2 = 128 - jax.random.randint(jax.random.fold_in(_rk, 8), (16,), 0, max(1, 128 // 4) + 1, jnp.int32)
        _ctx_4096P = jax.random.normal(jax.random.fold_in(_rk, 11), (16, 16, 1024), jnp.float32)
        _ctx_4096c = jax.random.dirichlet(jax.random.fold_in(_rk, 511), 0.3 * jnp.ones((16,), jnp.float32), (16, 128))
        _ctx_4096t = jnp.einsum('bsk,bkd->bsd', _ctx_4096c, _ctx_4096P)
        _ctx_4096t = _ctx_4096t * jax.lax.rsqrt(jnp.mean(jnp.square(_ctx_4096t)) + 1e-12) * 0.953939
        ctx_4096 = -2.6191e-05 + 0.999952 * (_ctx_4096t + 0.3 * jax.random.normal(jax.random.fold_in(_rk, 611), (16, 128, 1024), jnp.float32))
        _g = jax.random.normal(jax.random.fold_in(_rk, 9001), (2, 1), jnp.float32)
        _g = jnp.sign(_g) * jnp.maximum(jnp.abs(_g), 1.0) + (_g == 0) * 1.0
        g_xattn = _g[0]
        g_ffn = _g[1]
        return (x, ctx_4096, g_xattn, g_ffn)
    x, ctx_4096, g_xattn, g_ffn = _rec_inputs()

    def _L0_xattn_setup():
        import jax, jax.numpy as jnp
        import numpy as np
        TEXT_DIM = 1024
        FEATURE_DIM = 1024

        def _xavier_uniform(key, shape):
            fan_in, fan_out = (shape[1], shape[0])
            limit = float(np.sqrt(6.0 / (fan_in + fan_out)))
            return jax.random.uniform(key, shape, jnp.float32, -limit, limit)
        key = jax.random.key(seed)
        k1, k2, k3, k4 = jax.random.split(key, 4)
        text = jax.random.normal(k1, (8, 512, TEXT_DIM), jnp.float32)
        features = jax.random.normal(k2, (8, 144, FEATURE_DIM), jnp.float32)
        Wq = _xavier_uniform(k3, (FEATURE_DIM, TEXT_DIM))
        bq = jnp.zeros((FEATURE_DIM,), jnp.float32)
        Wk = _xavier_uniform(k4, (FEATURE_DIM, FEATURE_DIM))
        bk = jnp.zeros((FEATURE_DIM,), jnp.float32)
        return {'text': text, 'features': features, 'Wq': Wq, 'bq': bq, 'Wk': Wk, 'bk': bk}
    _L0_xattn_all = _L0_xattn_setup()
    _L0_xattn_in = {k: v for k, v in _L0_xattn_all.items() if k in ('Wq', 'bq', 'Wk', 'bk')}
    del _L0_xattn_all

    def _L0_ffn_setup():
        import jax, jax.numpy as jnp
        import numpy as np
        IN_F = 1024
        OUT_F = 1024
        RANK = 8
        NUM_EXPERTS = 64
        TOP_K = 16
        ROUTER_DIM = 16
        ALPHA = 32
        SCALING = ALPHA / TOP_K
        BOTTLENECK = NUM_EXPERTS * RANK
        key = jax.random.key(seed)
        ks = jax.random.split(key, 5)
        x = jax.random.normal(ks[0], (4, 1024, IN_F), dtype=jnp.float32)
        bound_a = float(np.sqrt(6.0 / IN_F))
        A_w = jax.random.uniform(ks[1], (BOTTLENECK, IN_F), jnp.float32, -bound_a, bound_a)
        B_w = jax.random.normal(ks[2], (OUT_F, BOTTLENECK), dtype=jnp.float32) * 0.02
        Wq_w = jax.random.normal(ks[3], (ROUTER_DIM, IN_F), dtype=jnp.float32) * 0.02
        keys = jax.random.normal(ks[4], (NUM_EXPERTS, ROUTER_DIM), dtype=jnp.float32) * 0.01
        return {'x': x, 'A_w': A_w, 'B_w': B_w, 'Wq_w': Wq_w, 'keys': keys}
    _L0_ffn_all = _L0_ffn_setup()
    _L0_ffn_in = {k: v for k, v in _L0_ffn_all.items() if k in ('A_w', 'B_w', 'Wq_w', 'keys')}
    del _L0_ffn_all
    return {'x': x, 'ctx_4096': ctx_4096, 'g_xattn': g_xattn, 'g_ffn': g_ffn, 'L0_xattn_Wq': _L0_xattn_in['Wq'], 'L0_xattn_bq': _L0_xattn_in['bq'], 'L0_xattn_Wk': _L0_xattn_in['Wk'], 'L0_xattn_bk': _L0_xattn_in['bk'], 'L0_ffn_A_w': _L0_ffn_in['A_w'], 'L0_ffn_B_w': _L0_ffn_in['B_w'], 'L0_ffn_Wq_w': _L0_ffn_in['Wq_w'], 'L0_ffn_keys': _L0_ffn_in['keys']}

def reference(x, ctx_4096, g_xattn, g_ffn, L0_xattn_Wq, L0_xattn_bq, L0_xattn_Wk, L0_xattn_bk, L0_ffn_A_w, L0_ffn_B_w, L0_ffn_Wq_w, L0_ffn_keys):
    import jax
    import jax.numpy as jnp

    def _L0_xattn_ref(text, features, Wq, bq, Wk, bk):
        import jax, jax.numpy as jnp
        import numpy as np
        TEXT_DIM = 1024
        FEATURE_DIM = 1024

        def _xavier_uniform(key, shape):
            fan_in, fan_out = (shape[1], shape[0])
            limit = float(np.sqrt(6.0 / (fan_in + fan_out)))
            return jax.random.uniform(key, shape, jnp.float32, -limit, limit)
        Q = jnp.einsum('btx,dx->btd', text, Wq) + bq
        K = jnp.einsum('bpx,dx->bpd', features, Wk) + bk
        scale = 1.0 / jnp.sqrt(jnp.asarray(K.shape[-1], K.dtype))
        scores = jnp.einsum('btd,bpd->btp', Q, K) * scale
        attn = jax.nn.softmax(scores, axis=-1)
        attended = jnp.einsum('btp,bpd->btd', attn, features)
        return attended

    def _L0_ffn_ref(x, A_w, B_w, Wq_w, keys):
        import jax, jax.numpy as jnp
        import numpy as np
        IN_F = 1024
        OUT_F = 1024
        RANK = 8
        NUM_EXPERTS = 64
        TOP_K = 16
        ROUTER_DIM = 16
        ALPHA = 32
        SCALING = ALPHA / TOP_K
        BOTTLENECK = NUM_EXPERTS * RANK
        q = jnp.einsum('bsd,rd->bsr', x, Wq_w)
        scores = jnp.einsum('bsr,er->bse', q, keys)
        top_vals, top_idx = jax.lax.top_k(scores, TOP_K)
        top_w = jax.nn.softmax(top_vals, axis=-1)
        gate = jnp.sum(jax.nn.one_hot(top_idx, NUM_EXPERTS, dtype=top_w.dtype) * top_w[..., None], axis=-2)
        z = jnp.einsum('bsd,nd->bsn', x, A_w)
        z = z.reshape(*z.shape[:-1], NUM_EXPERTS, RANK)
        z_gated = (z * gate[..., None]).reshape(*z.shape[:-2], BOTTLENECK)
        out = jnp.einsum('bsn,on->bso', z_gated, B_w) * SCALING
        return out
    x = x + jnp.tanh(g_xattn[0]) * _L0_xattn_ref(_layernorm(x, axis=-1), ctx_4096, L0_xattn_Wq, L0_xattn_bq, L0_xattn_Wk, L0_xattn_bk)
    x = x + jnp.tanh(g_ffn[0]) * _L0_ffn_ref(_layernorm(x, axis=-1), L0_ffn_A_w, L0_ffn_B_w, L0_ffn_Wq_w, L0_ffn_keys)
    return x

_drawn_inputs = setup_inputs


def setup_inputs(seed=0):
    import zlib

    import numpy as np

    out = dict(_drawn_inputs(seed))
    spreads = {'L0_xattn_bq': (0.0, 0.52), 'L0_xattn_bk': (0.0, 0.8)}
    factors = {}
    for name, (base, spread) in spreads.items():
        noise = np.random.default_rng([zlib.crc32(name.encode()), seed]).standard_normal(out[name].shape)
        drawn = base * np.exp(spread * noise) if base else spread * noise
        out[name] = jnp.asarray(drawn.astype(out[name].dtype))
    for name, factor in factors.items():
        out[name] = (out[name] * factor).astype(out[name].dtype)
    return out
```

```python
import concourse.bass as bass
from concourse import mybir
from contextlib import ExitStack


class SelfSync:

    def __init__(self, eng, sem):
        self.eng, self.sem, self.n = eng, sem, 0

    def restart(self):
        self.eng.sem_clear(self.sem)
        self.n = 0

    def done(self, ins):
        self.n += 1
        ins.then_inc(self.sem, 1)
        self.eng.wait_ge(self.sem, self.n)


def gated_xattn_moe(nc, x, x_t, ctx, ctx_t, smalls, ident_d, wq_d, wk_d, a_t, b_t, router_w, keys_t, out):
    f32, f32r, i32 = mybir.dt.float32, mybir.dt.float32r, mybir.dt.int32
    ALU, ACT, AX = mybir.AluOpType, mybir.ActivationFunctionType, mybir.AxisListType

    P = 128
    T, D = x.shape
    KD = D // P
    GT = 512
    NG = T // GT
    JB = GT // P
    NT = T // P
    H2 = D // 2
    NB = b_t.shape[0]
    KB = NB // P
    NE = keys_t.shape[1]
    RANK = NB // NE
    RD = keys_t.shape[0]
    ZC = NB // 2 + NE // 2
    SCALE = float(D) ** -0.5
    SCALING = 32 / 16
    EPS = 1e-5
    LOW = -3e38
    MAGIC = float(0x5F3759DF)

    x1_d = nc.dram_tensor("x1_scratch", (T, D), f32, kind="Internal").ap()

    ctx_mgr = ExitStack()
    with ctx_mgr:
        def sem(name):
            return ctx_mgr.enter_context(nc.semaphore(name))

        def persistent(name, shape, dt):
            return ctx_mgr.enter_context(nc.sbuf_tensor(name, shape, dt))

        class Region:

            def __init__(self):
                self.stack = ExitStack()

            def tensor(self, name, shape, dt):
                return self.stack.enter_context(nc.sbuf_tensor(name, shape, dt))

            def again(self):
                self.stack.close()
                self.stack = ExitStack()

        ident = persistent("ident", [P, P], f32)
        ones = persistent("ones", [P, P], f32)
        small = persistent("small", [P, 2 * KD + 2], f32)
        bq_c, bk_c = small[:, 0:KD], small[:, KD:2 * KD]
        tanh_g = persistent("tanh_g", [P, 2], f32)
        neg_mean_w = persistent("neg_mean_w", [P, KD], f32)
        bn = persistent("bn", [P, 12], f32)
        mv = persistent("mv", [P, 2], f32)
        uk = persistent("uk", [P, KD + 1], f32)
        kb_part = persistent("kb_part", [P, 1], f32)
        kb_junk = persistent("kb_junk", [P, KD], f32)
        c_cols = persistent("c_cols", [P, JB], f32)
        rstd = persistent("rstd", [P, 4], f32)
        row_max = persistent("row_max", [P, 1], f32)
        neg_max = persistent("neg_max", [P, 2], f32)
        row_sum = persistent("row_sum", [P, 2], f32)
        att_scale = persistent("att_scale", [P, 2], f32)
        nmr = persistent("nmr", [P, 1], f32)
        top8 = persistent("top8", [P, 16], f32)
        neg_top = persistent("neg_top", [P, 1], f32)
        gate_sum = persistent("gate_sum", [P, 2], f32)
        gate_scale = persistent("gate_scale", [P, 4], f32)
        acc_u = persistent("acc_u", [P, D], f32)
        v_bc = persistent("v_bc", [P, D], f32)

        r_m = Region()
        mt = r_m.tensor("mt", [P, 2, KD, D], f32r)
        r_1 = Region()
        wq = r_1.tensor("wq", [P, 2, KD, D], f32r)
        r_2 = Region()
        wk = r_2.tensor("wk", [P, 2, 2, H2], f32r)
        wq_raw = r_2.tensor("wq_raw", [P, 2, D], f32)
        wk_raw = r_2.tensor("wk_raw", [P, 2, H2], f32)
        r_3 = Region()
        ct = r_3.tensor("ct", [P, 2, KD, GT], f32r)
        ct_raw = r_3.tensor("ct_raw", [P, KD, GT], f32)

        r_3.again()
        bt = r_3.tensor("bt", [P, 2, KB, D], f32r)
        bt_raw1 = r_3.tensor("bt_raw1", [P, KB // 2, D], f32)
        rw = r_3.tensor("rw", [RD, D], f32)
        kt = r_3.tensor("kt", [RD, NE], f32)

        r_3.again(), r_2.again()
        cn = r_2.tensor("cn", [P, 2, D], f32r)
        at = r_2.tensor("at", [P, 2, P], f32r)
        c_bc = r_2.tensor("c_bc", [P, GT], f32)
        logits = r_2.tensor("logits", [P, 2, P], f32)
        probs = r_2.tensor("probs", [P, 2, P], f32)

        r_2.again(), r_1.again()
        gbuf = r_1.tensor("gbuf", [P, KD, GT], f32)
        xt = r_1.tensor("xt", [P, KD, GT], f32)
        x_nat = r_1.tensor("x_nat", [P, JB, D], f32)
        c_nat = r_1.tensor("c_nat", [P, JB, D], f32)
        r_1.again()
        x1 = r_1.tensor("x1", [P, 4, D], f32)
        xn = r_1.tensor("xn", [P, D], f32)
        xnt = r_1.tensor("xnt", [P, 2, KD, P], f32r)
        zg = r_1.tensor("zg", [P, NB], f32)
        gate = r_1.tensor("gate", [P, NE], f32)
        sc = r_1.tensor("sc", [P, 4, NE], f32)
        r_1.tensor("pad", [P, 2 * KD * GT + JB * D - 4 * D - D - 2 * KD * P - NB - 5 * NE], f32)
        zgt = r_1.tensor("zgt", [P, 2, KB, P], f32r)

        r_1.again(), r_m.again()
        art = r_m.tensor("art", [P, 2, KD, 2, ZC], f32r)
        at_raw = r_m.tensor("at_raw", [P, KD, NB], f32)
        bt_raw0 = r_m.tensor("bt_raw0", [P, KB // 2, D], f32)
        r_m.again()

        ps = ctx_mgr.enter_context(nc.psum_tensor("ps", [P, 8, 512], f32))

        const_in, ident_in, rk_in = sem("const_in"), sem("ident_in"), sem("rk_in")
        wq_in = [sem(f"wq_in{i}") for i in range(2)]
        wk_in = [sem(f"wk_in{i}") for i in range(2)]
        ones_set, tanh_done = sem("ones_set"), sem("tanh_done")
        mean_done, wq_hi, wq_lo = sem("mean_done"), sem("wq_hi"), sem("wq_lo")
        wk_hi, wk_lo, wk_used = sem("wk_hi"), sem("wk_lo"), sem("wk_used")
        mt_done, mt_hi, mt_lo = sem("mt_done"), sem("mt_hi"), sem("mt_lo")
        uv_ready, uv_done, uk_set, v_set = sem("uv_ready"), sem("uv_done"), sem("uk_set"), sem("v_set")
        ct_in = [sem(f"ct_in{i}") for i in range(2)]
        ct_hi, ct_lo = sem("ct_hi"), sem("ct_lo")
        g_done, g_set = sem("g_done"), sem("g_set")
        xt_in = sem("xt_in")
        x_in = [sem(f"x_in{i}") for i in range(JB)]
        c_in = [sem(f"c_in{i}") for i in range(JB)]
        c_done, sc_done, cb_set = sem("c_done"), sem("sc_done"), sem("cb_set")
        max_done, exp_done = sem("max_done"), sem("exp_done")
        at_done, at_hi, at_lo = sem("at_done"), sem("at_hi"), sem("at_lo")
        cn_hi, cn_lo = sem("cn_hi"), sem("cn_lo")
        att_done, x1_done = sem("att_done"), sem("x1_done")
        x1_st = [sem(f"x1_st{i}") for i in range(JB)]
        a_in = sem("a_in")
        b_in = [sem(f"b_in{i}") for i in range(2)]
        r_done, ab_hi, ab_lo = sem("r_done"), sem("ab_hi"), sem("ab_lo")
        x1_in = [sem(f"x1_in{i}") for i in range(4)]
        ln_done, xn_set = sem("ln_done"), sem("xn_set")
        xt_done, xt_hi, xt_lo = sem("xt_done"), sem("xt_hi"), sem("xt_lo")
        z_done, top_done, e_done, zg_set = sem("z_done"), sem("top_done"), sem("e_done"), sem("zg_set")
        zt_done, zt_hi, zt_lo = sem("zt_done"), sem("zt_hi"), sem("zt_lo")
        o_done, fin_set = sem("o_done"), sem("fin_set")
        out_st = [sem(f"out_st{i}") for i in range(4)]
        dve_self = sem("dve_self")

        block = ctx_mgr.enter_context(nc.Block())

        def f(ap):
            return ap.bitcast(f32)

        @block.sync
        def _(sp):
            sp.dma_start(small[:], smalls).then_inc(const_in, 16)

            def load_wk(n):
                if n >= 2:
                    sp.wait_ge(wk_lo, n - 1)
                half, k = divmod(n, KD)
                sp.dma_start(wk_raw[:, n % 2, :], wk_d[k * P:(k + 1) * P, half * H2:(half + 1) * H2])\
                    .then_inc(wk_in[n % 2], 16)

            for k in range(KD):
                if k >= 2:
                    sp.wait_ge(wq_lo, k - 1)
                sp.dma_start(wq_raw[:, k % 2, :], wq_d[k * P:(k + 1) * P, :]).then_inc(wq_in[k % 2], 16)
                load_wk(k)
                if k == 0:
                    sp.dma_start(ident[:], ident_d).then_inc(ident_in, 16)

            def load_ct(g, h):
                sp.dma_start(ct_raw[:, h * 4:(h + 1) * 4, :],
                             ctx_t[h * H2:(h + 1) * H2, bass.ds(g * GT, GT)].rearrange("(k p) t -> p k t", p=P))\
                    .then_inc(ct_in[h], 16)

            load_ct(0, 0)
            load_ct(0, 1)
            for n in range(KD, 2 * KD):
                load_wk(n)
            sp.wait_ge(mt_done, 16)

            def load_xt(g):
                sp.dma_start(xt[:], x_t[:, bass.ds(g * GT, GT)].rearrange("(k p) t -> p k t", p=P))\
                    .then_inc(xt_in, 16)

            def load_c(g, j):
                sp.dma_start(c_nat[:, j, :], ctx[bass.ds(g * GT + j * P, P), :]).then_inc(c_in[j], 16)

            def load_x(g, j):
                sp.dma_start(x_nat[:, j, :], x[bass.ds(g * GT + j * P, P), :]).then_inc(x_in[j], 16)

            for j in range(JB):
                load_c(0, j)
            load_xt(0)
            for h in range(2):
                sp.wait_ge(ct_lo, 4 * (h + 1))
                load_ct(1, h)
            for j in range(JB):
                load_x(0, j)

            def group(g, more_ct, more):
                if more_ct:
                    for h in range(2):
                        sp.wait_ge(ct_lo, g * KD + (KD + 4 * (h + 1)))
                        load_ct(g + 2, h)
                if more:
                    sp.wait_ge(sc_done, g * JB + JB)
                    load_xt(g + 1)
                for j in range(JB):
                    if more:
                        sp.wait_ge(cn_lo, g * JB + (j + 1))
                        load_c(g + 1, j)
                    sp.wait_ge(x1_done, g * JB + (j + 1))
                    sp.dma_start(x1_d[bass.ds(g * GT + j * P, P), :], x_nat[:, j, :]).then_inc(x1_st[j], 16)
                    if more and j >= 1:
                        sp.wait_ge(x1_st[j - 1], g * 16 + 16)
                        load_x(g + 1, j - 1)
                if more:
                    sp.wait_ge(x1_st[JB - 1], g * 16 + 16)
                    load_x(g + 1, JB - 1)

            with sp.Fori(0, NG - 2) as g:
                group(g, True, True)
            group(NG - 2, False, True)

            sp.wait_ge(g_done, NG * KD)
            sp.dma_start(at_raw[:], a_t.rearrange("(k p) n -> p k n", p=P)).then_inc(a_in, 16)
            sp.dma_start(rw[:], router_w).then_inc(rk_in, 16)
            sp.dma_start(kt[:], keys_t).then_inc(rk_in, 16)
            for h, raw in enumerate((bt_raw0, bt_raw1)):
                sp.dma_start(raw[:], b_t[h * (NB // 2):(h + 1) * (NB // 2), :].rearrange("(k p) n -> p k n", p=P))\
                    .then_inc(b_in[h], 16)

            def load_x1(t, slot):
                sp.dma_start(x1[:, slot, :], x1_d[bass.ds(t * P, P), :]).then_inc(x1_in[slot], 16)

            sp.wait_ge(sc_done, NT)
            for t in range(4):
                load_x1(t, t)
            group(NG - 1, False, False)
            for j in range(JB):
                sp.wait_ge(x1_st[j], 16 * NG)

            def store_out(t, u):
                sp.wait_ge(fin_set, t + 1)
                sp.dma_start(out[bass.ds(t * P, P), :], x1[:, u, :]).then_inc(out_st[u], 16)

            store_out(0, 0)
            with sp.Fori(0, 3) as i:
                for w in range(4):
                    store_out(i * 4 + (w + 1), (w + 1) % 4)
                    sp.wait_ge(out_st[w], i * 16 + 16)
                    load_x1(i * 4 + (w + 4), w)
            for t in range(NT - 3, NT):
                store_out(t, t % 4)
            for u in range(4):
                sp.wait_ge(out_st[u], 16 * (NT // 4))

        @block.gpsimd
        def _(pool):
            pool.memset(ones[:], 1.0).then_inc(ones_set, 1)

        @block.scalar
        def _(act):
            act.wait_ge(const_in, 16)
            nc.scalar.activation(tanh_g[:], small[:, 2 * KD:2 * KD + 2], ACT.Tanh).then_inc(tanh_done, 1)

            def split_wk(n):
                act.wait_ge(wk_in[n % 2], 16 * (n // 2 + 1))
                if n >= 2:
                    act.wait_ge(wk_used, n - 1)
                nc.scalar.activation(wk[:, n % 2, 0, :], wk_raw[:, n % 2, :], ACT.Copy).then_inc(wk_hi, 1)

            def evac_mt(p, b):
                act.wait_ge(mt_done, 8 * p + b + 1)
                nc.scalar.activation(mt[:, 0, 4 * p + b // 2, (b % 2) * H2:(b % 2 + 1) * H2], ps[:, b, :],
                                     ACT.Copy).then_inc(mt_hi, 1)

            for k in range(KD):
                split_wk(k)
                act.wait_ge(mean_done, k + 1)
                nc.scalar.activation(wq[:, 0, k, :], wq_raw[:, k % 2, :], ACT.Identity,
                                     bias=neg_mean_w[:, k:k + 1]).then_inc(wq_hi, 1)
            split_wk(KD)
            for b in range(8):
                evac_mt(0, b)
                if b == 3:
                    split_wk(KD + 1)

            def split_ct(g, k):
                act.wait_ge(ct_in[k // 4], g * 16 + 16)
                nc.scalar.activation(ct[:, 0, k, :], ct_raw[:, k, :], ACT.Copy).then_inc(ct_hi, 1)

            for n in range(KD + 2, 2 * KD):
                split_wk(n)
                split_ct(0, n - (KD + 2))
            for k in (KD - 2, KD - 1):
                split_ct(0, k)
            for b in range(8):
                evac_mt(1, b)

            def evac_g(g, i):
                act.wait_ge(g_done, g * KD + (i + 1))
                nc.scalar.activation(gbuf[:, i, :], ps[:, i % 2, :], ACT.Identity, bias=uk[:, i:i + 1])\
                    .then_inc(g_set, 1)

            act.wait_ge(uv_done, 1)
            nc.scalar.activation(uk[:], ps[:, 2, 0:KD + 1], ACT.Copy).then_inc(uk_set, 1)
            act.wait_ge(uk_set, 1)
            for i in range(KD):
                evac_g(0, i)

            def group(g, more):
                if more:
                    act.wait_ge(g_done, g * KD + KD)
                    for k in range(KD):
                        split_ct(g + 1, k)
                act.wait_ge(sc_done, g * JB + JB)
                nc.scalar.activation(c_bc[:], ps[:, 3, :], ACT.Identity, bias=uk[:, KD:KD + 1]).then_inc(cb_set, 1)

                def exp(j):
                    act.wait_ge(max_done, g * JB + (j + 1))
                    nc.scalar.activation(probs[:, j % 2, :], logits[:, j % 2, :], ACT.Exp,
                                         bias=neg_max[:, j % 2:j % 2 + 1], scale=SCALE,
                                         accum_out=row_sum[:, j % 2:j % 2 + 1]).then_inc(exp_done, 1)

                exp(0)
                for j in range(JB):
                    if more:
                        evac_g(g + 1, 2 * j)
                    act.wait_ge(at_done, g * JB + (j + 1))
                    nc.scalar.activation(at[:, 0, :], ps[:, 4, j * P:(j + 1) * P], ACT.Copy).then_inc(at_hi, 1)
                    act.wait_ge(c_in[j], g * 16 + 16)
                    nc.scalar.activation(cn[:, 0, :], c_nat[:, j, :], ACT.Copy).then_inc(cn_hi, 1)
                    if j + 1 < JB:
                        exp(j + 1)
                    if more:
                        evac_g(g + 1, 2 * j + 1)

            with act.Fori(0, NG - 1) as g:
                group(g, True)
            group(NG - 1, False)

            act.wait_ge(a_in, 16)
            for k in range(0, KD, 2):
                for kk in (k, k + 1):
                    last = nc.scalar.activation(art[:, 0, kk, :, 0:NB // 2],
                                                at_raw[:, kk, :].rearrange("p (c n) -> p c n", c=2), ACT.Copy)
                last.then_inc(ab_hi, 1)
            act.wait_ge(r_done, 1)
            nc.scalar.activation(art[:, 0, :, :, NB // 2:ZC],
                                 ps[:, 7, :].rearrange("p (k c e) -> p k c e", k=KD, c=2), ACT.Copy)\
                .then_inc(ab_hi, 1)

            def split_b():
                for h, raw in enumerate((bt_raw0, bt_raw1)):
                    act.wait_ge(b_in[h], 16)
                    for k in range(KB // 2):
                        nc.scalar.activation(bt[:, 0, h * (KB // 2) + k, :], raw[:, k, :], ACT.Copy)\
                            .then_inc(ab_hi, 1)

            def normalize(s, u):
                act.wait_ge(ln_done, s + 1)
                nc.scalar.activation(xn[:], x1[:, u, :], ACT.Identity, bias=nmr[:], scale=rstd[:, 0:1])\
                    .then_inc(xn_set, 1)

            def split_xt(s):
                for h in range(2):
                    act.wait_ge(xt_done, s * 2 + (h + 1))
                    nc.scalar.activation(xnt[:, 0, 4 * h:4 * h + 4, :].rearrange("p k t -> p (k t)"),
                                         ps[:, 2 + h, :], ACT.Copy).then_inc(xt_hi, 1)

            def split_zt(s):
                act.wait_ge(zt_done, s + 1)
                nc.scalar.activation(zgt[:, 0, :, :].rearrange("p k t -> p (k t)"), ps[:, 4, :], ACT.Copy)\
                    .then_inc(zt_hi, 1)

            def exp_top(s):
                act.wait_ge(top_done, s + 1)
                nc.scalar.activation(sc[:, 3, :], sc[:, 0, :], ACT.Exp, bias=neg_top[:]).then_inc(e_done, 1)

            normalize(0, 0)
            split_xt(0)
            split_b()
            normalize(1, 1)
            exp_top(0)
            split_xt(1)

            def tile(s, u):
                split_zt(s - 1)
                normalize(s + 1, (u + 1) % 4)
                exp_top(s)
                split_xt(s + 1)

            with act.Fori(0, 3) as i:
                for w in range(4):
                    tile(i * 4 + (w + 1), (w + 1) % 4)
            for s in range(NT - 3, NT - 1):
                tile(s, s % 4)
            split_zt(NT - 2)
            exp_top(NT - 1)
            split_zt(NT - 1)

        @block.vector
        def _(dve):
            own = SelfSync(dve, dve_self)

            def tt(out_, a, b, op):
                return nc.vector.tensor_tensor(out_, a, b, op)

            def row_stats(src):
                nc.vector.bn_stats(bn[:, 0:6], src[:, 0:H2])
                own.done(nc.vector.bn_stats(bn[:, 6:12], src[:, H2:D]))
                return nc.vector.bn_aggr(mv[:], bn[:])

            def rstd_of_var():
                y, v, a, b = (rstd[:, c:c + 1] for c in range(4))
                own.done(nc.vector.tensor_scalar(v, mv[:, 1:2], EPS, None, ALU.add))
                own.done(nc.vector.tensor_scalar(a.bitcast(i32), v.bitcast(i32), 1, None, ALU.logical_shift_right))
                own.done(nc.vector.tensor_scalar(y.bitcast(i32), a.bitcast(i32), -1.0, MAGIC, ALU.mult, ALU.add))
                for _ in range(3):
                    own.done(nc.vector.scalar_tensor_tensor(a, y, v, y, ALU.mult, ALU.mult))
                    own.done(nc.vector.tensor_scalar(b, a, -0.5, 1.5, ALU.mult, ALU.add))
                    last = tt(y, y, b, ALU.mult)
                    if _ < 2:
                        own.done(last)
                return last

            def split_wk(n):
                half, k = divmod(n, KD)
                dve.wait_ge(wk_in[n % 2], 16 * (n // 2 + 1))
                vh = v_bc[:, half * H2:(half + 1) * H2]
                raw = wk_raw[:, n % 2, :]
                if k == 0:
                    nc.vector.tensor_scalar(vh, raw, bq_c[:, 0:1], None, ALU.mult).then_inc(dve_self, 1)
                else:
                    nc.vector.scalar_tensor_tensor(vh, raw, bq_c[:, k:k + 1], vh, ALU.mult, ALU.add)\
                        .then_inc(dve_self, 1)
                own.n += 1
                dve.wait_ge(wk_hi, n + 1)
                tt(wk[:, n % 2, 1, :], raw, f(wk[:, n % 2, 0, :]), ALU.subtract).then_inc(wk_lo, 1)
                dve.wait_ge(dve_self, own.n)

            def evac_mt(p, b):
                dve.wait_ge(mt_hi, 8 * p + b + 1)
                cols = slice((b % 2) * H2, (b % 2 + 1) * H2)
                tt(mt[:, 1, 4 * p + b // 2, cols], ps[:, b, :], f(mt[:, 0, 4 * p + b // 2, cols]), ALU.subtract)\
                    .then_inc(mt_lo, 1)

            dve.wait_ge(const_in, 16)
            for k in range(KD):
                raw = wq_raw[:, k % 2, :]
                dve.wait_ge(wq_in[k % 2], 16 * (k // 2 + 1))
                own.done(row_stats(raw))
                nc.vector.tensor_scalar(neg_mean_w[:, k:k + 1], mv[:, 0:1], -1.0, None, ALU.mult)\
                    .then_inc(mean_done, 1)
                if k == 0:
                    own.done(nc.vector.tensor_scalar(acc_u[:], raw, bk_c[:, 0:1], None, ALU.mult))
                split_wk(k)
                if k > 0:
                    own.done(nc.vector.scalar_tensor_tensor(acc_u[:], raw, bk_c[:, k:k + 1], acc_u[:],
                                                            ALU.mult, ALU.add))
                dve.wait_ge(wq_hi, k + 1)
                nc.vector.scalar_tensor_tensor(wq[:, 1, k, :], raw, neg_mean_w[:, k:k + 1], f(wq[:, 0, k, :]),
                                               ALU.add, ALU.subtract).then_inc(wq_lo, 1)
            own.done(nc.vector.tensor_tensor(kb_junk[:], bq_c, bk_c, ALU.mult))
            own.done(nc.vector.tensor_reduce(kb_part[:], kb_junk[:], AX.X, ALU.add))
            own.done(row_stats(acc_u))
            own.done(nc.vector.tensor_scalar(acc_u[:], acc_u[:], mv[:, 0:1], None, ALU.subtract))
            split_wk(KD)
            for b in range(8):
                evac_mt(0, b)
                if b == 3:
                    split_wk(KD + 1)

            def split_ct(g, k):
                dve.wait_ge(ct_hi, g * KD + (k + 1))
                tt(ct[:, 1, k, :], ct_raw[:, k, :], f(ct[:, 0, k, :]), ALU.subtract).then_inc(ct_lo, 1)

            for n in range(KD + 2, 2 * KD):
                split_wk(n)
                split_ct(0, n - (KD + 2))
            for k in (KD - 2, KD - 1):
                split_ct(0, k)
            nc.vector.tensor_copy(kb_junk[:, 0:1], kb_part[:]).then_inc(uv_ready, 1)
            for b in range(8):
                evac_mt(1, b)
            dve.wait_ge(uv_done, 1)
            own.done(nc.vector.tensor_copy(v_bc[:].rearrange("p (h n) -> p h n", h=2), ps[:, 5:7, :]))

            def c_column(g, j):
                dve.wait_ge(c_in[j], g * 16 + 16)
                if not (isinstance(g, int) and g == 0 and j == 0):
                    dve.wait_ge(c_done, g * JB + j)
                nc.vector.scalar_tensor_tensor(acc_u[:], c_nat[:, j, :], 1.0, v_bc[:], ALU.mult, ALU.mult,
                                               accum_out=c_cols[:, j:j + 1]).then_inc(c_done, 1)

            for j in range(JB):
                c_column(0, j)

            def group(g, more):
                if more:
                    for k in range(KD):
                        split_ct(g + 1, k)

                def softmax_head(j):
                    dve.wait_ge(x_in[j], g * 16 + 16)
                    own.done(row_stats(x_nat[:, j, :]))
                    own.done(rstd_of_var())
                    if j == 0:
                        dve.wait_ge(cb_set, g + 1)
                    if j >= 2:
                        dve.wait_ge(exp_done, g * JB + (j - 1))
                    own.done(nc.vector.scalar_tensor_tensor(
                        logits[:, j % 2, :], ps[:, 2, j * P:(j + 1) * P], rstd[:, 0:1],
                        c_bc[:, j * P:(j + 1) * P], ALU.mult, ALU.add))
                    own.done(nc.vector.tensor_reduce(row_max[:], logits[:, j % 2, :], AX.X, ALU.max))
                    nc.vector.tensor_scalar(neg_max[:, j % 2:j % 2 + 1], row_max[:], -SCALE, None, ALU.mult)\
                        .then_inc(max_done, 1)

                softmax_head(0)
                for j in range(JB):
                    dve.wait_ge(exp_done, g * JB + (j + 1))
                    own.done(nc.vector.reciprocal(att_scale[:, 0:1], row_sum[:, j % 2:j % 2 + 1]))
                    own.done(tt(att_scale[:, 1:2], att_scale[:, 0:1], tanh_g[:, 0:1], ALU.mult))
                    dve.wait_ge(at_hi, g * JB + (j + 1))
                    tt(at[:, 1, :], ps[:, 4, j * P:(j + 1) * P], f(at[:, 0, :]), ALU.subtract).then_inc(at_lo, 1)
                    dve.wait_ge(cn_hi, g * JB + (j + 1))
                    tt(cn[:, 1, :], c_nat[:, j, :], f(cn[:, 0, :]), ALU.subtract).then_inc(cn_lo, 1)
                    if j + 1 < JB:
                        softmax_head(j + 1)
                    if more and j >= 1:
                        c_column(g + 1, j - 1)
                    dve.wait_ge(att_done, g * JB + (j + 1))
                    nc.vector.scalar_tensor_tensor(
                        x_nat[:, j, :].rearrange("p (h n) -> p h n", h=2), ps[:, 5:7, :], att_scale[:, 1:2],
                        x_nat[:, j, :].rearrange("p (h n) -> p h n", h=2), ALU.mult, ALU.add).then_inc(x1_done, 1)
                if more:
                    c_column(g + 1, JB - 1)

            dve.wait_ge(tanh_done, 1)
            with dve.Fori(0, NG - 1) as g:
                own.restart()
                group(g, True)
            own.restart()
            group(NG - 1, False)

            for k in range(0, KD, 2):
                dve.wait_ge(ab_hi, k // 2 + 1)
                for kk in (k, k + 1):
                    last = tt(art[:, 1, kk, :, 0:NB // 2], at_raw[:, kk, :].rearrange("p (c n) -> p c n", c=2),
                              f(art[:, 0, kk, :, 0:NB // 2]), ALU.subtract)
                last.then_inc(ab_lo, 1)
            dve.wait_ge(ab_hi, 5)
            tt(art[:, 1, :, :, NB // 2:ZC], ps[:, 7, :].rearrange("p (k c e) -> p k c e", k=KD, c=2),
               f(art[:, 0, :, :, NB // 2:ZC]), ALU.subtract).then_inc(ab_lo, 1)

            def split_b():
                for h, raw in enumerate((bt_raw0, bt_raw1)):
                    for k in range(KB // 2):
                        dve.wait_ge(ab_hi, 6 + h * (KB // 2) + k)
                        tt(bt[:, 1, h * (KB // 2) + k, :], raw[:, k, :], f(bt[:, 0, h * (KB // 2) + k, :]),
                           ALU.subtract).then_inc(ab_lo, 1)

            def layer_norm(s, u, n):
                dve.wait_ge(x1_in[u], n)
                own.done(row_stats(x1[:, u, :]))
                own.done(rstd_of_var())
                nc.vector.scalar_tensor_tensor(nmr[:], mv[:, 0:1], -1.0, rstd[:, 0:1], ALU.mult, ALU.mult)\
                    .then_inc(ln_done, 1)

            def split_xt(s):
                for h in range(2):
                    dve.wait_ge(xt_hi, s * 2 + (h + 1))
                    tt(xnt[:, 1, 4 * h:4 * h + 4, :].rearrange("p k t -> p (k t)"), ps[:, 2 + h, :],
                       f(xnt[:, 0, 4 * h:4 * h + 4, :]).rearrange("p k t -> p (k t)"), ALU.subtract)\
                        .then_inc(xt_lo, 1)

            def split_zt(s):
                dve.wait_ge(zt_hi, s + 1)
                tt(zgt[:, 1, :, :].rearrange("p k t -> p (k t)"), ps[:, 4, :],
                   f(zgt[:, 0, :, :]).rearrange("p k t -> p (k t)"), ALU.subtract).then_inc(zt_lo, 1)

            def gates(s, u):
                dve.wait_ge(z_done, s + 1)
                own.done(nc.vector.tensor_copy(sc[:, 0, :].rearrange("p (c e) -> p c e", c=2),
                                               ps[:, 0:2, NB // 2:ZC]))
                own.done(nc.vector.max(top8[:, 0:8], sc[:, 0, :]))
                nc.vector.tensor_scalar(neg_top[:], top8[:, 0:1], -1.0, None, ALU.mult).then_inc(top_done, 1)
                own.done(nc.vector.match_replace(sc[:, 1, :], top8[:, 0:8], sc[:, 0, :], LOW))
                own.done(nc.vector.max(top8[:, 8:16], sc[:, 1, :]))
                own.done(nc.vector.match_replace(sc[:, 2, :], top8[:, 8:16], sc[:, 1, :], LOW))
                dve.wait_ge(e_done, s + 1)
                own.done(nc.vector.scalar_tensor_tensor(gate[:], sc[:, 2, :], LOW, sc[:, 3, :], ALU.is_equal,
                                                        ALU.mult, accum_out=gate_sum[:, 0:1]))
                nc.vector.tensor_tensor(
                    zg[:].rearrange("p (c e r) -> p c e r", c=2, r=RANK),
                    ps[:, 0:2, 0:NB // 2].rearrange("p c (e r) -> p c e r", r=RANK),
                    gate[:].rearrange("p (c e) -> p c e", c=2).unsqueeze(3).to_broadcast([P, 2, NE // 2, RANK]),
                    ALU.mult).then_inc(zg_set, 1)
                own.done(nc.vector.reciprocal(gate_sum[:, 1:2], gate_sum[:, 0:1]))
                own.done(nc.vector.scalar_tensor_tensor(gate_scale[:, u:u + 1], gate_sum[:, 1:2], SCALING,
                                                        tanh_g[:, 1:2], ALU.mult, ALU.mult))

            def finish(s, u):
                dve.wait_ge(o_done, s + 1)
                xu = x1[:, u, :].rearrange("p (h n) -> p h n", h=2)
                nc.vector.scalar_tensor_tensor(xu, ps[:, 5:7, :], gate_scale[:, u:u + 1], xu, ALU.mult, ALU.add)\
                    .then_inc(fin_set, 1)

            layer_norm(0, 0, 16)
            split_xt(0)
            split_b()
            dve.wait_ge(xn_set, 1)
            layer_norm(1, 1, 16)
            gates(0, 0)
            split_xt(1)

            def tile(s, u, n):
                split_zt(s - 1)
                dve.wait_ge(xn_set, s + 1)
                layer_norm(s + 1, (u + 1) % 4, n)
                gates(s, u)
                split_xt(s + 1)
                finish(s - 1, (u - 1) % 4)

            with dve.Fori(0, 3) as i:
                own.restart()
                for w in range(4):
                    tile(i * 4 + (w + 1), (w + 1) % 4, i * 16 + 16 * ((w + 2) // 4 + 1))
            own.restart()
            for s in range(NT - 3, NT - 1):
                tile(s, s % 4, 16 * ((s + 1) // 4 + 1))
            split_zt(NT - 2)
            gates(NT - 1, 3)
            finish(NT - 2, 2)
            split_zt(NT - 1)
            finish(NT - 1, 3)

        @block.tensor
        def _(pe):
            HILO = ((0, 0), (0, 1), (1, 0))

            for p in range(2):
                for k in range(KD):
                    n = p * KD + k
                    pe.wait_ge(wk_lo, n + 1)
                    if p == 0:
                        pe.wait_ge(wq_lo, k + 1)
                    for j in range(4):
                        for h in range(2):
                            b = 2 * j + h
                            if p and k == 0:
                                pe.wait_ge(mt_lo, b + 1)
                            for q, (a, c) in enumerate(HILO):
                                last = nc.tensor.matmul(ps[:, b, :], wk[:, n % 2, a, j * P:(j + 1) * P],
                                                        wq[:, c, k, h * H2:(h + 1) * H2],
                                                        start=(k == 0 and q == 0), stop=(k == KD - 1 and q == 2))
                            if k == KD - 1:
                                last.then_inc(mt_done, 1)
                    if k == KD - 1:
                        pe.wait_ge(mt_done, 8 * p + 8)
                        pe.sem_inc(wk_used, 1)
                    else:
                        last.then_inc(wk_used, 1)

            def g_chunk(g, i):
                if not isinstance(g, int) or g > 0:
                    pe.wait_ge(g_set, g * KD + (i - 1))
                elif i >= 2:
                    pe.wait_ge(g_set, i - 1)
                else:
                    pe.wait_ge(mt_lo, 8 + i + 1)
                for k in range(KD):
                    if i == 0:
                        pe.wait_ge(ct_lo, g * KD + (k + 1))
                        if isinstance(g, int) and g == 0 and k >= 4:
                            pe.wait_ge(mt_lo, 8 + 2 * (k - 4) + 1)
                    for q, (a, c) in enumerate(HILO):
                        last = nc.tensor.matmul(ps[:, i % 2, :], mt[:, a, k, i * P:(i + 1) * P], ct[:, c, k, :],
                                                start=(k == 0 and q == 0), stop=(k == KD - 1 and q == 2))
                last.then_inc(g_done, 1)

            g_chunk(0, 0)
            pe.wait_ge(uv_ready, 1)
            pe.wait_ge(ones_set, 1)
            pe.wait_ge(mt_lo, 16)
            for i in range(KD):
                nc.tensor.matmul(ps[:, 2, i:i + 1], acc_u[:, i * P:(i + 1) * P], ones[:, 0:1], start=True, stop=True)
            nc.tensor.matmul(ps[:, 2, KD:KD + 1], ones[:], kb_part[:], start=True, stop=True)
            for h in range(2):
                last = nc.tensor.matmul(ps[:, 5 + h, :], ones[:], v_bc[:, h * H2:(h + 1) * H2], start=True, stop=True)
            last.then_inc(uv_done, 1)
            for i in range(1, KD):
                g_chunk(0, i)

            pe.wait_ge(ident_in, 16)

            def group(g, more):
                pe.wait_ge(xt_in, g * 16 + 16)
                pe.wait_ge(g_set, g * KD + KD)
                for j in range(JB):
                    cols = slice(j * P, (j + 1) * P)
                    for k in range(KD):
                        nc.tensor.matmul(ps[:, 2, cols], xt[:, k, cols], gbuf[:, k, cols],
                                         start=(k == 0), stop=(k == KD - 1))
                    pe.wait_ge(c_done, g * JB + (j + 1))
                    nc.tensor.matmul(ps[:, 3, cols], c_cols[:, j:j + 1].to_broadcast([P, P]), ident[:],
                                     start=True, stop=True).then_inc(sc_done, 1)
                if more:
                    g_chunk(g + 1, 0)
                for j in range(JB):
                    pe.wait_ge(exp_done, g * JB + (j + 1))
                    nc.tensor.transpose(ps[:, 4, j * P:(j + 1) * P], probs[:, j % 2, :], ident[:])\
                        .then_inc(at_done, 1)
                    if more:
                        g_chunk(g + 1, 2 * j + 1)
                    if j > 0:
                        pe.wait_ge(x1_done, g * JB + j)
                    pe.wait_ge(at_lo, g * JB + (j + 1))
                    pe.wait_ge(cn_lo, g * JB + (j + 1))
                    for h in range(2):
                        for q, (a, c) in enumerate(HILO):
                            last = nc.tensor.matmul(ps[:, 5 + h, :], at[:, a, :], cn[:, c, h * H2:(h + 1) * H2],
                                                    start=(q == 0), stop=(q == 2))
                    last.then_inc(att_done, 1)
                    if more and j + 1 < JB:
                        g_chunk(g + 1, 2 * j + 2)

            with pe.Fori(0, NG - 1) as g:
                group(g, True)
            group(NG - 1, False)

            pe.wait_ge(rk_in, 32)
            for k in range(KD):
                last = nc.tensor.matmul(ps[:, 7, k * NE:(k + 1) * NE], rw[:, k * P:(k + 1) * P], kt[:],
                                        start=True, stop=True)
            last.then_inc(r_done, 1)

            def transpose_x(s):
                pe.wait_ge(xn_set, s + 1)
                for h in range(2):
                    for k in range(4):
                        c = 4 * h + k
                        last = nc.tensor.transpose(ps[:, 2 + h, k * P:(k + 1) * P], xn[:, c * P:(c + 1) * P], ident[:])
                    last.then_inc(xt_done, 1)

            def experts_in(s, first=False):
                for k in range(KD):
                    if k % 4 == 0:
                        pe.wait_ge(xt_lo, s * 2 + (k // 4 + 1))
                    if first and k == 0:
                        pe.wait_ge(ab_lo, 5)
                    for q, (a, c) in enumerate(HILO):
                        for h in range(2):
                            last = nc.tensor.matmul(ps[:, h, 0:ZC], xnt[:, a, k, :], art[:, c, k, h, :],
                                                    start=(k == 0 and q == 0), stop=(k == KD - 1 and q == 2))
                last.then_inc(z_done, 1)

            def transpose_z(s):
                pe.wait_ge(zg_set, s + 1)
                for k in range(KB):
                    last = nc.tensor.transpose(ps[:, 4, k * P:(k + 1) * P], zg[:, k * P:(k + 1) * P], ident[:])
                last.then_inc(zt_done, 1)

            def experts_out(s, first=False):
                pe.wait_ge(zt_lo, s + 1)
                if first:
                    pe.wait_ge(ab_lo, 5 + KB)
                else:
                    pe.wait_ge(fin_set, s)
                for k in range(KB):
                    for q, (a, c) in enumerate(HILO):
                        for h in range(2):
                            last = nc.tensor.matmul(ps[:, 5 + h, :], zgt[:, a, k, :], bt[:, c, k, h * H2:(h + 1) * H2],
                                                    start=(k == 0 and q == 0), stop=(k == KB - 1 and q == 2))
                last.then_inc(o_done, 1)

            transpose_x(0)
            experts_in(0, True)
            transpose_x(1)
            transpose_z(0)

            def tile(s, first=False):
                experts_in(s)
                transpose_x(s + 1)
                experts_out(s - 1, first)
                transpose_z(s)

            tile(1, True)
            with pe.Fori(2, NT - 1) as s:
                tile(s)
            experts_in(NT - 1)
            experts_out(NT - 2)
            transpose_z(NT - 1)
            experts_out(NT - 1)


def kernel(x, ctx_4096, g_xattn, g_ffn, L0_xattn_Wq, L0_xattn_bq, L0_xattn_Wk, L0_xattn_bk,
           L0_ffn_A_w, L0_ffn_B_w, L0_ffn_Wq_w, L0_ffn_keys):
    import numpy as np
    import concourse.bacc as bacc
    from concourse.bass_utils import run_bass_kernel_spmd

    B, S, D = x.shape
    x2, c2 = np.reshape(x, (B * S, D)), np.reshape(ctx_4096, (B * S, D))

    def columns(v):
        return np.reshape(v, (-1, 128)).T

    smalls = np.concatenate([columns(L0_xattn_bq), columns(L0_xattn_bk),
                             np.broadcast_to(g_xattn, (128, 1)), np.broadcast_to(g_ffn, (128, 1))], axis=1)
    arrays = {
        "x": x2, "x_t": x2.T, "ctx": c2, "ctx_t": c2.T, "smalls": smalls,
        "ident": np.eye(128, dtype=np.float32), "wq": L0_xattn_Wq, "wk": L0_xattn_Wk,
        "a_t": np.transpose(L0_ffn_A_w), "b_t": np.transpose(L0_ffn_B_w), "router_w": L0_ffn_Wq_w,
        "keys_t": np.transpose(L0_ffn_keys),
    }
    arrays = {k: np.ascontiguousarray(v) for k, v in arrays.items()}
    nc = bacc.Bacc("TRN2", target_bir_lowering=False, num_devices=1)
    args = [nc.dram_tensor(f"in_{k}", v.shape, mybir.dt.from_np(v.dtype), kind="ExternalInput").ap()
            for k, v in arrays.items()]
    out = nc.dram_tensor("out_x", (B * S, D), mybir.dt.float32, kind="ExternalOutput").ap()
    gated_xattn_moe(nc, *args, out)
    r = run_bass_kernel_spmd(nc, [{f"in_{k}": v for k, v in arrays.items()}], core_ids=[0])
    return np.reshape(r.results[0]["out_x"], (B, S, D))
```

```python
import concourse.bass as bass
from concourse import mybir
from contextlib import ExitStack


class SelfSync:

    def __init__(self, eng, sem):
        self.eng, self.sem, self.n = eng, sem, 0

    def restart(self):
        self.eng.sem_clear(self.sem)
        self.n = 0

    def done(self, ins):
        self.n += 1
        ins.then_inc(self.sem, 1)
        self.eng.wait_ge(self.sem, self.n)


def gated_xattn_moe(nc, x, x_t, ctx, ctx_t, smalls, ident_d, wq_d, wk_d, a_t, b_t, router_w, keys_t, out):
    f32, f32r, i32 = mybir.dt.float32, mybir.dt.float32r, mybir.dt.int32
    ALU, ACT, AX = mybir.AluOpType, mybir.ActivationFunctionType, mybir.AxisListType

    P = 128
    T, D = x.shape
    KD = D // P
    GT = 512
    NG = T // GT
    JB = GT // P
    NT = T // P
    H2 = D // 2
    NB = b_t.shape[0]
    KB = NB // P
    NE = keys_t.shape[1]
    RANK = NB // NE
    RD = keys_t.shape[0]
    ZC = NB // 2 + NE // 2
    SCALE = float(D) ** -0.5
    SCALING = 32 / 16
    EPS = 1e-5
    LOW = -3e38
    MAGIC = float(0x5F3759DF)

    x1_d = nc.dram_tensor("x1_scratch", (T, D), f32, kind="Internal").ap()

    ctx_mgr = ExitStack()
    with ctx_mgr:
        def sem(name):
            return ctx_mgr.enter_context(nc.semaphore(name))

        def persistent(name, shape, dt):
            return ctx_mgr.enter_context(nc.sbuf_tensor(name, shape, dt))

        class Region:

            def __init__(self):
                self.stack = ExitStack()

            def tensor(self, name, shape, dt):
                return self.stack.enter_context(nc.sbuf_tensor(name, shape, dt))

            def again(self):
                self.stack.close()
                self.stack = ExitStack()

        ident = persistent("ident", [P, P], f32)
        ones = persistent("ones", [P, P], f32)
        small = persistent("small", [P, 2 * KD + 2], f32)
        bq_c, bk_c = small[:, 0:KD], small[:, KD:2 * KD]
        tanh_g = persistent("tanh_g", [P, 2], f32)
        neg_mean_w = persistent("neg_mean_w", [P, KD], f32)
        bn = persistent("bn", [P, 12], f32)
        mv = persistent("mv", [P, 2], f32)
        uk = persistent("uk", [P, KD + 1], f32)
        kb_part = persistent("kb_part", [P, 1], f32)
        kb_junk = persistent("kb_junk", [P, KD], f32)
        c_cols = persistent("c_cols", [P, JB], f32)
        rs = persistent("rs", [P, 4, JB], f32)
        rstd = rs[:, 0, 0:1]
        mv2 = persistent("mv2", [P, JB, 2], f32)
        ln2 = persistent("ln2", [P, 2, NT], f32)
        row_max = persistent("row_max", [P, 1], f32)
        neg_max = persistent("neg_max", [P, 2], f32)
        row_sum = persistent("row_sum", [P, 2], f32)
        att_scale = persistent("att_scale", [P, 2], f32)
        top8 = persistent("top8", [P, 16], f32)
        neg_top = persistent("neg_top", [P, 1], f32)
        gate_sum = persistent("gate_sum", [P, 2], f32)
        gate_scale = persistent("gate_scale", [P, 4], f32)
        acc_u = persistent("acc_u", [P, D], f32)
        v_bc = persistent("v_bc", [P, D], f32)

        r_m = Region()
        mt = r_m.tensor("mt", [P, 2, KD, D], f32r)
        r_1 = Region()
        wq = r_1.tensor("wq", [P, 2, KD, D], f32r)
        r_2 = Region()
        wk = r_2.tensor("wk", [P, 2, 2, H2], f32r)
        wq_raw = r_2.tensor("wq_raw", [P, 2, D], f32)
        wk_raw = r_2.tensor("wk_raw", [P, 2, H2], f32)
        r_3 = Region()
        ct = r_3.tensor("ct", [P, 2, KD, GT], f32r)
        ct_raw = r_3.tensor("ct_raw", [P, KD, GT], f32)

        r_3.again()
        bt = r_3.tensor("bt", [P, 2, KB, D], f32r)
        bt_raw1 = r_3.tensor("bt_raw1", [P, KB // 2, D], f32)
        rw = r_3.tensor("rw", [RD, D], f32)
        kt = r_3.tensor("kt", [RD, NE], f32)

        r_3.again(), r_2.again()
        cn = r_2.tensor("cn", [P, 2, D], f32r)
        at = r_2.tensor("at", [P, 2, P], f32r)
        c_bc = r_2.tensor("c_bc", [P, GT], f32)
        logits = r_2.tensor("logits", [P, 2, P], f32)
        probs = r_2.tensor("probs", [P, 2, P], f32)

        r_2.again(), r_1.again()
        gbuf = r_1.tensor("gbuf", [P, KD, GT], f32)
        xt = r_1.tensor("xt", [P, KD, GT], f32)
        x_nat = r_1.tensor("x_nat", [P, JB, D], f32)
        c_nat = r_1.tensor("c_nat", [P, JB, D], f32)
        r_1.again()
        x1_3 = r_1.tensor("x1_3", [P, D], f32)
        bt_raw0 = r_1.tensor("bt_raw0", [P, KB // 2, D], f32)
        r_1.tensor("pad_g", [P, KD * GT - 3 * D], f32)
        xn = r_1.tensor("xn", [P, D], f32)
        xnt = r_1.tensor("xnt", [P, 2, KD, P], f32r)
        zg = r_1.tensor("zg", [P, NB], f32)
        gate = r_1.tensor("gate", [P, NE], f32)
        sc = r_1.tensor("sc", [P, 4, NE], f32)
        r_1.tensor("pad_x", [P, KD * GT + JB * D - D - 2 * KD * P - NB - 5 * NE], f32)
        zgt = r_1.tensor("zgt", [P, 2, KB, P], f32r)

        r_1.again(), r_m.again()
        art = r_m.tensor("art", [P, 2, KD, 2, ZC], f32r)
        at_raw = r_m.tensor("at_raw", [P, KD, NB], f32)
        x1 = [r_m.tensor(f"x1_{i}", [P, D], f32) for i in range(3)] + [x1_3]
        r_m.again()

        ps = ctx_mgr.enter_context(nc.psum_tensor("ps", [P, 8, 512], f32))

        const_in, ident_in, rk_in = sem("const_in"), sem("ident_in"), sem("rk_in")
        wq_in = [sem(f"wq_in{i}") for i in range(2)]
        wk_in = [sem(f"wk_in{i}") for i in range(2)]
        ones_set, tanh_done = sem("ones_set"), sem("tanh_done")
        mean_done, wq_hi, wq_lo = sem("mean_done"), sem("wq_hi"), sem("wq_lo")
        wk_hi, wk_lo, wk_used = sem("wk_hi"), sem("wk_lo"), sem("wk_used")
        mt_done, mt_hi, mt_lo = sem("mt_done"), sem("mt_hi"), sem("mt_lo")
        uv_ready, uv_done, uk_set, v_set = sem("uv_ready"), sem("uv_done"), sem("uk_set"), sem("v_set")
        ct_in = [sem(f"ct_in{i}") for i in range(2)]
        ct_hi, ct_lo = sem("ct_hi"), sem("ct_lo")
        g_done, g_set = sem("g_done"), sem("g_set")
        xt_in = sem("xt_in")
        x_in = [sem(f"x_in{i}") for i in range(JB)]
        c_in = [sem(f"c_in{i}") for i in range(JB)]
        c_done, sc_done, cb_set = sem("c_done"), sem("sc_done"), sem("cb_set")
        max_done, exp_done = sem("max_done"), sem("exp_done")
        at_done, at_hi, at_lo = sem("at_done"), sem("at_hi"), sem("at_lo")
        cn_hi, cn_lo = sem("cn_hi"), sem("cn_lo")
        att_done, x1_done, x1_stats = sem("att_done"), sem("x1_done"), sem("x1_stats")
        x1_st = [sem(f"x1_st{i}") for i in range(JB)]
        a_in = [sem(f"a_in{i}") for i in range(2)]
        b_in = [sem(f"b_in{i}") for i in range(2)]
        r_done, ar_hi, ar_lo, b_hi, b_lo = (sem(n) for n in ("r_done", "ar_hi", "ar_lo", "b_hi", "b_lo"))
        x1_in = [sem(f"x1_in{i}") for i in range(4)]
        ln2_set, xn_set = sem("ln2_set"), sem("xn_set")
        xt_done, xt_hi, xt_lo = sem("xt_done"), sem("xt_hi"), sem("xt_lo")
        z_done, top_done, e_done, zg_set = sem("z_done"), sem("top_done"), sem("e_done"), sem("zg_set")
        zt_done, zt_hi, zt_lo = sem("zt_done"), sem("zt_hi"), sem("zt_lo")
        o_done, fin_set = sem("o_done"), sem("fin_set")
        out_st = [sem(f"out_st{i}") for i in range(4)]
        dve_self = sem("dve_self")

        block = ctx_mgr.enter_context(nc.Block())

        def f(ap):
            return ap.bitcast(f32)

        @block.sync
        def _(sp):
            sp.dma_start(small[:], smalls).then_inc(const_in, 16)

            def load_wk(n):
                if n >= 2:
                    sp.wait_ge(wk_lo, n - 1)
                half, k = divmod(n, KD)
                sp.dma_start(wk_raw[:, n % 2, :], wk_d[k * P:(k + 1) * P, half * H2:(half + 1) * H2])\
                    .then_inc(wk_in[n % 2], 16)

            for k in range(KD):
                if k >= 2:
                    sp.wait_ge(wq_lo, k - 1)
                sp.dma_start(wq_raw[:, k % 2, :], wq_d[k * P:(k + 1) * P, :]).then_inc(wq_in[k % 2], 16)
                load_wk(k)
                if k == 0:
                    sp.dma_start(ident[:], ident_d).then_inc(ident_in, 16)

            def load_ct(g, h):
                sp.dma_start(ct_raw[:, h * 4:(h + 1) * 4, :],
                             ctx_t[h * H2:(h + 1) * H2, bass.ds(g * GT, GT)].rearrange("(k p) t -> p k t", p=P))\
                    .then_inc(ct_in[h], 16)

            load_ct(0, 0)
            load_ct(0, 1)
            for n in range(KD, 2 * KD):
                load_wk(n)
            sp.wait_ge(mt_done, 16)

            def load_xt(g):
                sp.dma_start(xt[:], x_t[:, bass.ds(g * GT, GT)].rearrange("(k p) t -> p k t", p=P))\
                    .then_inc(xt_in, 16)

            def load_c(g, j):
                sp.dma_start(c_nat[:, j, :], ctx[bass.ds(g * GT + j * P, P), :]).then_inc(c_in[j], 16)

            def load_x(g, j):
                sp.dma_start(x_nat[:, j, :], x[bass.ds(g * GT + j * P, P), :]).then_inc(x_in[j], 16)

            for j in range(JB):
                load_c(0, j)
            load_xt(0)
            for h in range(2):
                sp.wait_ge(ct_lo, 4 * (h + 1))
                load_ct(1, h)
            for j in range(JB):
                load_x(0, j)

            def group(g, more_ct):
                if more_ct:
                    for h in range(2):
                        sp.wait_ge(ct_lo, g * KD + (KD + 4 * (h + 1)))
                        load_ct(g + 2, h)
                sp.wait_ge(sc_done, g * JB + JB)
                load_xt(g + 1)
                for j in range(JB):
                    sp.wait_ge(cn_lo, g * JB + (j + 1))
                    load_c(g + 1, j)
                    sp.wait_ge(x1_done, g * JB + (j + 1))
                    sp.dma_start(x1_d[bass.ds(g * GT + j * P, P), :], x_nat[:, j, :]).then_inc(x1_st[j], 16)
                    if j >= 1:
                        sp.wait_ge(x1_st[j - 1], g * 16 + 16)
                        sp.wait_ge(x1_stats, g * JB + j)
                        load_x(g + 1, j - 1)
                sp.wait_ge(x1_st[JB - 1], g * 16 + 16)
                sp.wait_ge(x1_stats, g * JB + JB)
                load_x(g + 1, JB - 1)

            with sp.Fori(0, NG - 2) as g:
                group(g, True)
            group(NG - 2, False)

            def load_x1(t, slot):
                sp.dma_start(x1[slot][:], x1_d[bass.ds(t * P, P), :]).then_inc(x1_in[slot], 16)

            sp.wait_ge(g_done, NG * KD)
            load_x1(0, 0)
            for h in range(2):
                sp.dma_start(at_raw[:, 4 * h:4 * h + 4, :],
                             a_t[h * H2:(h + 1) * H2, :].rearrange("(k p) n -> p k n", p=P)).then_inc(a_in[h], 16)
            sp.dma_start(rw[:], router_w).then_inc(rk_in, 16)
            sp.dma_start(kt[:], keys_t).then_inc(rk_in, 16)
            load_x1(1, 1)
            sp.wait_ge(sc_done, NT)
            for h, raw in enumerate((bt_raw0, bt_raw1)):
                sp.dma_start(raw[:], b_t[h * (NB // 2):(h + 1) * (NB // 2), :].rearrange("(k p) n -> p k n", p=P))\
                    .then_inc(b_in[h], 16)
            load_x1(2, 2)
            load_x1(3, 3)

            def store_out(t, u):
                sp.wait_ge(fin_set, t + 1)
                sp.dma_start(out[bass.ds(t * P, P), :], x1[u][:]).then_inc(out_st[u], 16)

            def next_tile(t, u, n):
                sp.wait_ge(out_st[u], n)
                load_x1(t + 4, u)

            for j in range(JB):
                sp.wait_ge(x1_done, (NG - 1) * JB + j + 1)
                sp.dma_start(x1_d[(NG - 1) * GT + j * P:(NG - 1) * GT + (j + 1) * P, :], x_nat[:, j, :])\
                    .then_inc(x1_st[j], 16)
                if j >= 1:
                    store_out(j - 1, j - 1)
                    next_tile(j - 1, j - 1, 16)
            for j in range(JB):
                sp.wait_ge(x1_st[j], 16 * NG)
            with sp.Fori(0, 2) as i:
                for w in range(4):
                    u = (w + 3) % 4
                    store_out(i * 4 + (w + 3), u)
                    next_tile(i * 4 + (w + 3), u, i * 16 + 16 * ((w + 3) // 4 + 1))
            store_out(NT - 5, 3)
            next_tile(NT - 5, 3, 16 * (NT // 4 - 1))
            for t in range(NT - 4, NT):
                store_out(t, t % 4)
            for u in range(4):
                sp.wait_ge(out_st[u], 16 * (NT // 4))

        @block.gpsimd
        def _(pool):
            pool.memset(ones[:], 1.0).then_inc(ones_set, 1)

            def split_c(g, j):
                pool.wait_ge(cn_hi, g * JB + (j + 1))
                nc.gpsimd.tensor_tensor(cn[:, 1, :], c_nat[:, j, :], f(cn[:, 0, :]), ALU.subtract)\
                    .then_inc(cn_lo, 1)

            with pool.Fori(0, NG - 1) as g:
                for j in range(JB):
                    split_c(g, j)
            split_c(NG - 1, 0)
            for k in range(KB):
                raw = (bt_raw0, bt_raw1)[k // (KB // 2)]
                pool.wait_ge(b_hi, k + 1)
                nc.gpsimd.tensor_tensor(bt[:, 1, k, :], raw[:, k % (KB // 2), :], f(bt[:, 0, k, :]), ALU.subtract)\
                    .then_inc(b_lo, 1)
            for j in range(1, JB):
                split_c(NG - 1, j)

        @block.scalar
        def _(act):
            act.wait_ge(const_in, 16)
            nc.scalar.activation(tanh_g[:], small[:, 2 * KD:2 * KD + 2], ACT.Tanh).then_inc(tanh_done, 1)

            def split_wk(n):
                act.wait_ge(wk_in[n % 2], 16 * (n // 2 + 1))
                if n >= 2:
                    act.wait_ge(wk_used, n - 1)
                nc.scalar.activation(wk[:, n % 2, 0, :], wk_raw[:, n % 2, :], ACT.Copy).then_inc(wk_hi, 1)

            def evac_mt(p, b):
                act.wait_ge(mt_done, 8 * p + b + 1)
                nc.scalar.activation(mt[:, 0, 4 * p + b // 2, (b % 2) * H2:(b % 2 + 1) * H2], ps[:, b, :],
                                     ACT.Copy).then_inc(mt_hi, 1)

            for k in range(KD):
                split_wk(k)
                act.wait_ge(mean_done, k + 1)
                nc.scalar.activation(wq[:, 0, k, :], wq_raw[:, k % 2, :], ACT.Identity,
                                     bias=neg_mean_w[:, k:k + 1]).then_inc(wq_hi, 1)
            split_wk(KD)
            for b in range(8):
                evac_mt(0, b)
                if b == 3:
                    split_wk(KD + 1)

            def split_ct(g, k):
                act.wait_ge(ct_in[k // 4], g * 16 + 16)
                nc.scalar.activation(ct[:, 0, k, :], ct_raw[:, k, :], ACT.Copy).then_inc(ct_hi, 1)

            for n in range(KD + 2, 2 * KD):
                split_wk(n)
                split_ct(0, n - (KD + 2))
            for k in (KD - 2, KD - 1):
                split_ct(0, k)
            for b in range(8):
                evac_mt(1, b)

            def evac_g(g, i):
                act.wait_ge(g_done, g * KD + (i + 1))
                nc.scalar.activation(gbuf[:, i, :], ps[:, i % 2, :], ACT.Identity, bias=uk[:, i:i + 1])\
                    .then_inc(g_set, 1)

            act.wait_ge(uv_done, 1)
            nc.scalar.activation(uk[:], ps[:, 2, 0:KD + 1], ACT.Copy).then_inc(uk_set, 1)
            act.wait_ge(uk_set, 1)
            for i in range(KD):
                evac_g(0, i)

            def exp(g, j):
                act.wait_ge(max_done, g * JB + (j + 1))
                nc.scalar.activation(probs[:, j % 2, :], logits[:, j % 2, :], ACT.Exp,
                                     bias=neg_max[:, j % 2:j % 2 + 1], scale=SCALE,
                                     accum_out=row_sum[:, j % 2:j % 2 + 1]).then_inc(exp_done, 1)

            def split_at(g, j):
                act.wait_ge(at_done, g * JB + (j + 1))
                nc.scalar.activation(at[:, 0, :], ps[:, 7, j * P:(j + 1) * P], ACT.Copy).then_inc(at_hi, 1)

            def split_c(g, j):
                act.wait_ge(c_in[j], g * 16 + 16)
                if j > 0:
                    act.wait_ge(att_done, g * JB + j)
                nc.scalar.activation(cn[:, 0, :], c_nat[:, j, :], ACT.Copy).then_inc(cn_hi, 1)

            def group_head(g):
                act.wait_ge(sc_done, g * JB + JB)
                nc.scalar.activation(c_bc[:], ps[:, 3, :], ACT.Identity, bias=uk[:, KD:KD + 1]).then_inc(cb_set, 1)
                split_c(g, 0)
                exp(g, 0)

            with act.Fori(0, NG - 1) as g:
                act.wait_ge(g_done, g * KD + KD)
                for k in range(KD):
                    split_ct(g + 1, k)
                group_head(g)
                for j in range(JB):
                    evac_g(g + 1, 2 * j)
                    split_at(g, j)
                    if j + 1 < JB:
                        exp(g, j + 1)
                    evac_g(g + 1, 2 * j + 1)
                    if j + 1 < JB:
                        split_c(g, j + 1)

            def split_a(k):
                act.wait_ge(a_in[k // 4], 16)
                for kk in (k, k + 1):
                    last = nc.scalar.activation(art[:, 0, kk, :, 0:NB // 2],
                                                at_raw[:, kk, :].rearrange("p (c n) -> p c n", c=2), ACT.Copy)
                last.then_inc(ar_hi, 1)

            def split_b(k):
                h = k // (KB // 2)
                act.wait_ge(b_in[h], 16)
                nc.scalar.activation(bt[:, 0, k, :], (bt_raw0, bt_raw1)[h][:, k % (KB // 2), :], ACT.Copy)\
                    .then_inc(b_hi, 1)

            def normalize(t, u, n):
                act.wait_ge(x1_in[u], n)
                nc.scalar.activation(xn[:], x1[u][:], ACT.Identity, bias=ln2[:, 1, bass.ds(t, 1)],
                                     scale=ln2[:, 0, bass.ds(t, 1)]).then_inc(xn_set, 1)

            def split_xt(s):
                for h in range(2):
                    act.wait_ge(xt_done, s * 2 + (h + 1))
                    nc.scalar.activation(xnt[:, 0, 4 * h:4 * h + 4, :].rearrange("p k t -> p (k t)"),
                                         ps[:, 2 + h, :], ACT.Copy).then_inc(xt_hi, 1)

            def split_zt(s):
                act.wait_ge(zt_done, s + 1)
                nc.scalar.activation(zgt[:, 0, :, :].rearrange("p k t -> p (k t)"), ps[:, 4, :], ACT.Copy)\
                    .then_inc(zt_hi, 1)

            def exp_top(s):
                act.wait_ge(top_done, s + 1)
                nc.scalar.activation(sc[:, 3, :], sc[:, 0, :], ACT.Exp, bias=neg_top[:]).then_inc(e_done, 1)

            last_g = NG - 1
            act.wait_ge(ln2_set, NG - 1)
            group_head(last_g)
            normalize(0, 0, 16)
            split_a(0)
            split_xt(0)
            split_at(last_g, 0)
            for k in range(2, KD, 2):
                split_a(k)
            act.wait_ge(r_done, 1)
            nc.scalar.activation(art[:, 0, :, :, NB // 2:ZC],
                                 ps[:, 1, :].rearrange("p (k c e) -> p k c e", k=KD, c=2), ACT.Copy)\
                .then_inc(ar_hi, 1)
            exp(last_g, 1)
            for s in range(JB):
                if s >= 1:
                    split_zt(s - 1)
                    split_at(last_g, s)
                    if s + 1 < JB:
                        exp(last_g, s + 1)
                normalize(s + 1, (s + 1) % 4, 16 * ((s + 1) // 4 + 1))
                if s == 0:
                    for k in range(KB):
                        split_b(k)
                if s + 1 < JB:
                    split_c(last_g, s + 1)
                exp_top(s)
                split_xt(s + 1)

            def tile(s, u, n):
                split_zt(s - 1)
                normalize(s + 1, u, n)
                exp_top(s)
                split_xt(s + 1)

            with act.Fori(0, 2) as i:
                for w in range(4):
                    if w == 3:
                        act.wait_ge(ln2_set, i + 3)
                    tile(i * 4 + (w + 4), (w + 1) % 4, i * 16 + 16 * ((w + 5) // 4 + 1))
            for s in range(NT - 4, NT - 1):
                tile(s, (s + 1) % 4, 16 * ((s + 1) // 4 + 1))
            split_zt(NT - 2)
            exp_top(NT - 1)
            split_zt(NT - 1)

        @block.vector
        def _(dve):
            own = SelfSync(dve, dve_self)

            def tt(out_, a, b, op):
                return nc.vector.tensor_tensor(out_, a, b, op)

            def row_stats(src, to=mv[:]):
                nc.vector.bn_stats(bn[:, 0:6], src[:, 0:H2])
                own.done(nc.vector.bn_stats(bn[:, 6:12], src[:, H2:D]))
                return nc.vector.bn_aggr(to, bn[:])

            def rstd_of(var, w):
                y, v, h, a = (rs[:, c, 0:w] for c in range(4))
                nc.vector.tensor_scalar(h, var, -0.5, -0.5 * EPS, ALU.mult, ALU.add)
                own.done(nc.vector.tensor_scalar(v, var, EPS, None, ALU.add))
                own.done(nc.vector.tensor_scalar(a.bitcast(i32), v.bitcast(i32), 1, None, ALU.logical_shift_right))
                own.done(nc.vector.tensor_scalar(y.bitcast(i32), a.bitcast(i32), -1.0, MAGIC, ALU.mult, ALU.add))
                for step in range(3):
                    if w == 1:
                        own.done(nc.vector.scalar_tensor_tensor(a, y, h, y, ALU.mult, ALU.mult))
                    else:
                        own.done(tt(a, y, y, ALU.mult))
                        own.done(tt(a, a, h, ALU.mult))
                    own.done(nc.vector.scalar_tensor_tensor(y, a, 1.5, y, ALU.add, ALU.mult))

            def split_wk(n):
                half, k = divmod(n, KD)
                dve.wait_ge(wk_in[n % 2], 16 * (n // 2 + 1))
                vh = v_bc[:, half * H2:(half + 1) * H2]
                raw = wk_raw[:, n % 2, :]
                if k == 0:
                    nc.vector.tensor_scalar(vh, raw, bq_c[:, 0:1], None, ALU.mult).then_inc(dve_self, 1)
                else:
                    nc.vector.scalar_tensor_tensor(vh, raw, bq_c[:, k:k + 1], vh, ALU.mult, ALU.add)\
                        .then_inc(dve_self, 1)
                own.n += 1
                dve.wait_ge(wk_hi, n + 1)
                tt(wk[:, n % 2, 1, :], raw, f(wk[:, n % 2, 0, :]), ALU.subtract).then_inc(wk_lo, 1)
                dve.wait_ge(dve_self, own.n)

            def evac_mt(p, b):
                dve.wait_ge(mt_hi, 8 * p + b + 1)
                cols = slice((b % 2) * H2, (b % 2 + 1) * H2)
                tt(mt[:, 1, 4 * p + b // 2, cols], ps[:, b, :], f(mt[:, 0, 4 * p + b // 2, cols]), ALU.subtract)\
                    .then_inc(mt_lo, 1)

            dve.wait_ge(const_in, 16)
            for k in range(KD):
                raw = wq_raw[:, k % 2, :]
                dve.wait_ge(wq_in[k % 2], 16 * (k // 2 + 1))
                own.done(row_stats(raw))
                nc.vector.tensor_scalar(neg_mean_w[:, k:k + 1], mv[:, 0:1], -1.0, None, ALU.mult)\
                    .then_inc(mean_done, 1)
                if k == 0:
                    own.done(nc.vector.tensor_scalar(acc_u[:], raw, bk_c[:, 0:1], None, ALU.mult))
                split_wk(k)
                if k > 0:
                    own.done(nc.vector.scalar_tensor_tensor(acc_u[:], raw, bk_c[:, k:k + 1], acc_u[:],
                                                            ALU.mult, ALU.add))
                dve.wait_ge(wq_hi, k + 1)
                nc.vector.scalar_tensor_tensor(wq[:, 1, k, :], raw, neg_mean_w[:, k:k + 1], f(wq[:, 0, k, :]),
                                               ALU.add, ALU.subtract).then_inc(wq_lo, 1)
            own.done(nc.vector.tensor_tensor(kb_junk[:], bq_c, bk_c, ALU.mult))
            own.done(nc.vector.tensor_reduce(kb_part[:], kb_junk[:], AX.X, ALU.add))
            own.done(row_stats(acc_u))
            own.done(nc.vector.tensor_scalar(acc_u[:], acc_u[:], mv[:, 0:1], None, ALU.subtract))
            split_wk(KD)
            for b in range(8):
                evac_mt(0, b)
                if b == 3:
                    split_wk(KD + 1)

            def split_ct(g, k):
                dve.wait_ge(ct_hi, g * KD + (k + 1))
                tt(ct[:, 1, k, :], ct_raw[:, k, :], f(ct[:, 0, k, :]), ALU.subtract).then_inc(ct_lo, 1)

            for n in range(KD + 2, 2 * KD):
                split_wk(n)
                split_ct(0, n - (KD + 2))
            for k in (KD - 2, KD - 1):
                split_ct(0, k)
            nc.vector.tensor_copy(kb_junk[:, 0:1], kb_part[:]).then_inc(uv_ready, 1)
            for b in range(8):
                evac_mt(1, b)
            dve.wait_ge(uv_done, 1)
            own.done(nc.vector.tensor_copy(v_bc[:].rearrange("p (h n) -> p h n", h=2), ps[:, 5:7, :]))

            def c_column(g, j):
                dve.wait_ge(c_in[j], g * 16 + 16)
                if not (isinstance(g, int) and g == 0 and j == 0):
                    dve.wait_ge(c_done, g * JB + j)
                nc.vector.scalar_tensor_tensor(acc_u[:], c_nat[:, j, :], 1.0, v_bc[:], ALU.mult, ALU.mult,
                                               accum_out=c_cols[:, j:j + 1]).then_inc(c_done, 1)

            for j in range(JB):
                c_column(0, j)

            def softmax_head(g, j):
                dve.wait_ge(x_in[j], g * 16 + 16)
                own.done(row_stats(x_nat[:, j, :]))
                rstd_of(mv[:, 1:2], 1)
                if j == 0:
                    dve.wait_ge(cb_set, g + 1)
                if j >= 2:
                    dve.wait_ge(exp_done, g * JB + (j - 1))
                own.done(nc.vector.scalar_tensor_tensor(
                    logits[:, j % 2, :], ps[:, 7, j * P:(j + 1) * P], rstd,
                    c_bc[:, j * P:(j + 1) * P], ALU.mult, ALU.add))
                own.done(nc.vector.tensor_reduce(row_max[:], logits[:, j % 2, :], AX.X, ALU.max))
                nc.vector.tensor_scalar(neg_max[:, j % 2:j % 2 + 1], row_max[:], -SCALE, None, ALU.mult)\
                    .then_inc(max_done, 1)

            def split_at(g, j):
                dve.wait_ge(at_hi, g * JB + (j + 1))
                tt(at[:, 1, :], ps[:, 7, j * P:(j + 1) * P], f(at[:, 0, :]), ALU.subtract).then_inc(at_lo, 1)
                own.done(nc.vector.reciprocal(att_scale[:, 0:1], row_sum[:, j % 2:j % 2 + 1]))
                own.done(tt(att_scale[:, 1:2], att_scale[:, 0:1], tanh_g[:, 0:1], ALU.mult))

            def add_attended(g, j, bank):
                dve.wait_ge(att_done, g * JB + (j + 1))
                xj = x_nat[:, j, :].rearrange("p (h n) -> p h n", h=2)
                nc.vector.scalar_tensor_tensor(xj, ps[:, bank:bank + 2, :], att_scale[:, 1:2], xj,
                                               ALU.mult, ALU.add).then_inc(x1_done, 1)
                dve.wait_ge(x1_done, g * JB + (j + 1))
                row_stats(x_nat[:, j, :], mv2[:, j, :]).then_inc(x1_stats, 1)
                dve.wait_ge(x1_stats, g * JB + (j + 1))

            def group_norms(g):
                rstd_of(mv2[:, :, 1], JB)
                nc.vector.tensor_copy(ln2[:, 0, bass.ds(g * JB, JB)], rs[:, 0, :])
                nc.vector.scalar_tensor_tensor(ln2[:, 1, bass.ds(g * JB, JB)], mv2[:, :, 0], -1.0, rs[:, 0, :],
                                               ALU.mult, ALU.mult).then_inc(ln2_set, 1)
                dve.wait_ge(ln2_set, g + 1)

            dve.wait_ge(tanh_done, 1)
            with dve.Fori(0, NG - 1) as g:
                own.restart()
                for k in range(KD):
                    split_ct(g + 1, k)
                softmax_head(g, 0)
                for j in range(JB):
                    split_at(g, j)
                    if j + 1 < JB:
                        softmax_head(g, j + 1)
                    if j >= 1:
                        c_column(g + 1, j - 1)
                    add_attended(g, j, 5)
                c_column(g + 1, JB - 1)
                group_norms(g)
            own.restart()

            def split_a(k):
                dve.wait_ge(ar_hi, k // 2 + 1)
                for kk in (k, k + 1):
                    last = tt(art[:, 1, kk, :, 0:NB // 2], at_raw[:, kk, :].rearrange("p (c n) -> p c n", c=2),
                              f(art[:, 0, kk, :, 0:NB // 2]), ALU.subtract)
                last.then_inc(ar_lo, 1)

            def split_xt(s):
                for h in range(2):
                    dve.wait_ge(xt_hi, s * 2 + (h + 1))
                    tt(xnt[:, 1, 4 * h:4 * h + 4, :].rearrange("p k t -> p (k t)"), ps[:, 2 + h, :],
                       f(xnt[:, 0, 4 * h:4 * h + 4, :]).rearrange("p k t -> p (k t)"), ALU.subtract)\
                        .then_inc(xt_lo, 1)

            def split_zt(s):
                dve.wait_ge(zt_hi, s + 1)
                tt(zgt[:, 1, :, :].rearrange("p k t -> p (k t)"), ps[:, 4, :],
                   f(zgt[:, 0, :, :]).rearrange("p k t -> p (k t)"), ALU.subtract).then_inc(zt_lo, 1)

            def gates(s, u):
                dve.wait_ge(z_done, s + 1)
                own.done(nc.vector.tensor_copy(sc[:, 0, :].rearrange("p (c e) -> p c e", c=2),
                                               ps[:, 0:2, NB // 2:ZC]))
                own.done(nc.vector.max(top8[:, 0:8], sc[:, 0, :]))
                nc.vector.tensor_scalar(neg_top[:], top8[:, 0:1], -1.0, None, ALU.mult).then_inc(top_done, 1)
                own.done(nc.vector.match_replace(sc[:, 1, :], top8[:, 0:8], sc[:, 0, :], LOW))
                own.done(nc.vector.max(top8[:, 8:16], sc[:, 1, :]))
                own.done(nc.vector.match_replace(sc[:, 2, :], top8[:, 8:16], sc[:, 1, :], LOW))
                dve.wait_ge(e_done, s + 1)
                own.done(nc.vector.scalar_tensor_tensor(gate[:], sc[:, 2, :], LOW, sc[:, 3, :], ALU.is_equal,
                                                        ALU.mult, accum_out=gate_sum[:, 0:1]))
                nc.vector.tensor_tensor(
                    zg[:].rearrange("p (c e r) -> p c e r", c=2, r=RANK),
                    ps[:, 0:2, 0:NB // 2].rearrange("p c (e r) -> p c e r", r=RANK),
                    gate[:].rearrange("p (c e) -> p c e", c=2).unsqueeze(3).to_broadcast([P, 2, NE // 2, RANK]),
                    ALU.mult).then_inc(zg_set, 1)
                own.done(nc.vector.reciprocal(gate_sum[:, 1:2], gate_sum[:, 0:1]))
                own.done(nc.vector.scalar_tensor_tensor(gate_scale[:, u:u + 1], gate_sum[:, 1:2], SCALING,
                                                        tanh_g[:, 1:2], ALU.mult, ALU.mult))

            def finish(s, u):
                dve.wait_ge(o_done, s + 1)
                xu = x1[u][:].rearrange("p (h n) -> p h n", h=2)
                nc.vector.scalar_tensor_tensor(xu, ps[:, 5:7, :], gate_scale[:, u:u + 1], xu, ALU.mult, ALU.add)\
                    .then_inc(fin_set, 1)

            last_g = NG - 1
            softmax_head(last_g, 0)
            split_a(0)
            split_xt(0)
            split_at(last_g, 0)
            for k in range(2, KD, 2):
                split_a(k)
            dve.wait_ge(ar_hi, KD // 2 + 1)
            tt(art[:, 1, :, :, NB // 2:ZC], ps[:, 1, :].rearrange("p (k c e) -> p k c e", k=KD, c=2),
               f(art[:, 0, :, :, NB // 2:ZC]), ALU.subtract).then_inc(ar_lo, 1)
            softmax_head(last_g, 1)
            for s in range(JB):
                if s >= 1:
                    split_zt(s - 1)
                    split_at(last_g, s)
                    if s + 1 < JB:
                        softmax_head(last_g, s + 1)
                add_attended(last_g, s, 2)
                gates(s, s % 4)
                split_xt(s + 1)
                if s >= 1:
                    finish(s - 1, (s - 1) % 4)
            group_norms(last_g)

            def tile(s, u):
                split_zt(s - 1)
                gates(s, u)
                split_xt(s + 1)
                finish(s - 1, (u - 1) % 4)

            with dve.Fori(0, 2) as i:
                own.restart()
                for w in range(4):
                    tile(i * 4 + (w + 4), w)
            own.restart()
            for s in range(NT - 4, NT - 1):
                tile(s, s % 4)
            split_zt(NT - 2)
            gates(NT - 1, 3)
            finish(NT - 2, 2)
            split_zt(NT - 1)
            finish(NT - 1, 3)

        @block.tensor
        def _(pe):
            HILO = ((0, 0), (0, 1), (1, 0))

            for p in range(2):
                for k in range(KD):
                    n = p * KD + k
                    pe.wait_ge(wk_lo, n + 1)
                    if p == 0:
                        pe.wait_ge(wq_lo, k + 1)
                    for j in range(4):
                        for h in range(2):
                            b = 2 * j + h
                            if p and k == 0:
                                pe.wait_ge(mt_lo, b + 1)
                            for q, (a, c) in enumerate(HILO):
                                last = nc.tensor.matmul(ps[:, b, :], wk[:, n % 2, a, j * P:(j + 1) * P],
                                                        wq[:, c, k, h * H2:(h + 1) * H2],
                                                        start=(k == 0 and q == 0), stop=(k == KD - 1 and q == 2))
                            if k == KD - 1:
                                last.then_inc(mt_done, 1)
                    if k == KD - 1:
                        pe.wait_ge(mt_done, 8 * p + 8)
                        pe.sem_inc(wk_used, 1)
                    else:
                        last.then_inc(wk_used, 1)

            def g_chunk(g, i):
                if not isinstance(g, int) or g > 0:
                    pe.wait_ge(g_set, g * KD + (i - 1))
                elif i >= 2:
                    pe.wait_ge(g_set, i - 1)
                else:
                    pe.wait_ge(mt_lo, 8 + i + 1)
                for k in range(KD):
                    if i == 0:
                        pe.wait_ge(ct_lo, g * KD + (k + 1))
                        if isinstance(g, int) and g == 0 and k >= 4:
                            pe.wait_ge(mt_lo, 8 + 2 * (k - 4) + 1)
                    for q, (a, c) in enumerate(HILO):
                        last = nc.tensor.matmul(ps[:, i % 2, :], mt[:, a, k, i * P:(i + 1) * P], ct[:, c, k, :],
                                                start=(k == 0 and q == 0), stop=(k == KD - 1 and q == 2))
                last.then_inc(g_done, 1)

            g_chunk(0, 0)
            pe.wait_ge(uv_ready, 1)
            pe.wait_ge(ones_set, 1)
            pe.wait_ge(mt_lo, 16)
            for i in range(KD):
                nc.tensor.matmul(ps[:, 2, i:i + 1], acc_u[:, i * P:(i + 1) * P], ones[:, 0:1], start=True, stop=True)
            nc.tensor.matmul(ps[:, 2, KD:KD + 1], ones[:], kb_part[:], start=True, stop=True)
            for h in range(2):
                last = nc.tensor.matmul(ps[:, 5 + h, :], ones[:], v_bc[:, h * H2:(h + 1) * H2], start=True, stop=True)
            last.then_inc(uv_done, 1)
            for i in range(1, KD):
                g_chunk(0, i)

            pe.wait_ge(ident_in, 16)

            def scores(g):
                pe.wait_ge(xt_in, g * 16 + 16)
                pe.wait_ge(g_set, g * KD + KD)
                for j in range(JB):
                    cols = slice(j * P, (j + 1) * P)
                    for k in range(KD):
                        nc.tensor.matmul(ps[:, 7, cols], xt[:, k, cols], gbuf[:, k, cols],
                                         start=(k == 0), stop=(k == KD - 1))
                    pe.wait_ge(c_done, g * JB + (j + 1))
                    nc.tensor.matmul(ps[:, 3, cols], c_cols[:, j:j + 1].to_broadcast([P, P]), ident[:],
                                     start=True, stop=True).then_inc(sc_done, 1)

            def transpose_probs(g, j):
                pe.wait_ge(exp_done, g * JB + (j + 1))
                nc.tensor.transpose(ps[:, 7, j * P:(j + 1) * P], probs[:, j % 2, :], ident[:]).then_inc(at_done, 1)

            def attend(g, j, bank):
                pe.wait_ge(at_lo, g * JB + (j + 1))
                pe.wait_ge(cn_lo, g * JB + (j + 1))
                for h in range(2):
                    for q, (a, c) in enumerate(HILO):
                        last = nc.tensor.matmul(ps[:, bank + h, :], at[:, a, :], cn[:, c, h * H2:(h + 1) * H2],
                                                start=(q == 0), stop=(q == 2))
                last.then_inc(att_done, 1)

            with pe.Fori(0, NG - 1) as g:
                scores(g)
                g_chunk(g + 1, 0)
                for j in range(JB):
                    transpose_probs(g, j)
                    g_chunk(g + 1, 2 * j + 1)
                    if j > 0:
                        pe.wait_ge(x1_done, g * JB + j)
                    attend(g, j, 5)
                    if j + 1 < JB:
                        g_chunk(g + 1, 2 * j + 2)
            scores(NG - 1)

            pe.wait_ge(rk_in, 32)
            for k in range(KD):
                last = nc.tensor.matmul(ps[:, 1, k * NE:(k + 1) * NE], rw[:, k * P:(k + 1) * P], kt[:],
                                        start=True, stop=True)
            last.then_inc(r_done, 1)

            def transpose_x(s):
                pe.wait_ge(xn_set, s + 1)
                for h in range(2):
                    for k in range(4):
                        c = 4 * h + k
                        last = nc.tensor.transpose(ps[:, 2 + h, k * P:(k + 1) * P], xn[:, c * P:(c + 1) * P], ident[:])
                    last.then_inc(xt_done, 1)

            def experts_in(s, ks=range(KD), first=False):
                for k in ks:
                    if k % 4 == 0:
                        pe.wait_ge(xt_lo, s * 2 + (k // 4 + 1))
                    if first and k == 0:
                        pe.wait_ge(ar_lo, KD // 2 + 1)
                    for q, (a, c) in enumerate(HILO):
                        for h in range(2):
                            last = nc.tensor.matmul(ps[:, h, 0:ZC], xnt[:, a, k, :], art[:, c, k, h, :],
                                                    start=(k == 0 and q == 0), stop=(k == KD - 1 and q == 2))
                if ks[-1] == KD - 1:
                    last.then_inc(z_done, 1)

            def transpose_z(s):
                pe.wait_ge(zg_set, s + 1)
                for k in range(KB):
                    last = nc.tensor.transpose(ps[:, 4, k * P:(k + 1) * P], zg[:, k * P:(k + 1) * P], ident[:])
                last.then_inc(zt_done, 1)

            def experts_out(s, first=False):
                pe.wait_ge(zt_lo, s + 1)
                if first:
                    pe.wait_ge(b_lo, KB)
                else:
                    pe.wait_ge(fin_set, s)
                for k in range(KB):
                    for q, (a, c) in enumerate(HILO):
                        for h in range(2):
                            last = nc.tensor.matmul(ps[:, 5 + h, :], zgt[:, a, k, :], bt[:, c, k, h * H2:(h + 1) * H2],
                                                    start=(k == 0 and q == 0), stop=(k == KB - 1 and q == 2))
                last.then_inc(o_done, 1)

            last_g = NG - 1
            transpose_x(0)
            transpose_probs(last_g, 0)
            for s in range(JB):
                experts_in(s, range(KD // 2), first=(s == 0))
                pe.wait_ge(xt_lo, s * 2 + 2)
                attend(last_g, s, 2)
                experts_in(s, range(KD // 2, KD))
                pe.wait_ge(x1_done, last_g * JB + s + 1)
                transpose_x(s + 1)
                if s >= 1:
                    experts_out(s - 1, first=(s == 1))
                if s + 1 < JB:
                    transpose_probs(last_g, s + 1)
                transpose_z(s)

            with pe.Fori(JB, NT - 1) as s:
                experts_in(s)
                transpose_x(s + 1)
                experts_out(s - 1)
                transpose_z(s)
            experts_in(NT - 1)
            experts_out(NT - 2)
            transpose_z(NT - 1)
            experts_out(NT - 1)


def kernel(x, ctx_4096, g_xattn, g_ffn, L0_xattn_Wq, L0_xattn_bq, L0_xattn_Wk, L0_xattn_bk,
           L0_ffn_A_w, L0_ffn_B_w, L0_ffn_Wq_w, L0_ffn_keys):
    import numpy as np
    import concourse.bacc as bacc
    from concourse.bass_utils import run_bass_kernel_spmd

    B, S, D = x.shape
    x2, c2 = np.reshape(x, (B * S, D)), np.reshape(ctx_4096, (B * S, D))

    def columns(v):
        return np.reshape(v, (-1, 128)).T

    smalls = np.concatenate([columns(L0_xattn_bq), columns(L0_xattn_bk),
                             np.broadcast_to(g_xattn, (128, 1)), np.broadcast_to(g_ffn, (128, 1))], axis=1)
    arrays = {
        "x": x2, "x_t": x2.T, "ctx": c2, "ctx_t": c2.T, "smalls": smalls,
        "ident": np.eye(128, dtype=np.float32), "wq": L0_xattn_Wq, "wk": L0_xattn_Wk,
        "a_t": np.transpose(L0_ffn_A_w), "b_t": np.transpose(L0_ffn_B_w), "router_w": L0_ffn_Wq_w,
        "keys_t": np.transpose(L0_ffn_keys),
    }
    arrays = {k: np.ascontiguousarray(v) for k, v in arrays.items()}
    nc = bacc.Bacc("TRN2", target_bir_lowering=False, num_devices=1)
    args = [nc.dram_tensor(f"in_{k}", v.shape, mybir.dt.from_np(v.dtype), kind="ExternalInput").ap()
            for k, v in arrays.items()]
    out = nc.dram_tensor("out_x", (B * S, D), mybir.dt.float32, kind="ExternalOutput").ap()
    gated_xattn_moe(nc, *args, out)
    r = run_bass_kernel_spmd(nc, [{f"in_{k}": v for k, v in arrays.items()}], core_ids=[0])
    return np.reshape(r.results[0]["out_x"], (B, S, D))
```

```python
import concourse.bass as bass
from concourse import mybir
from contextlib import ExitStack


class SelfSync:

    def __init__(self, eng, sem):
        self.eng, self.sem, self.n = eng, sem, 0

    def restart(self):
        self.eng.sem_clear(self.sem)
        self.n = 0

    def done(self, ins):
        self.n += 1
        ins.then_inc(self.sem, 1)
        self.eng.wait_ge(self.sem, self.n)


def gated_xattn_moe(nc, x, x_t, ctx, ctx_t, smalls, ident_d, wq_d, wk_d, a_t, b_t, router_w, keys_t, out):
    f32, f32r, i32 = mybir.dt.float32, mybir.dt.float32r, mybir.dt.int32
    ALU, ACT, AX = mybir.AluOpType, mybir.ActivationFunctionType, mybir.AxisListType

    P = 128
    T, D = x.shape
    KD = D // P
    GT = 512
    NG = T // GT
    JB = GT // P
    NT = T // P
    H2 = D // 2
    NB = b_t.shape[0]
    KB = NB // P
    NE = keys_t.shape[1]
    RANK = NB // NE
    RD = keys_t.shape[0]
    ZC = NB // 2 + NE // 2
    SCALE = float(D) ** -0.5
    SCALING = 32 / 16
    EPS = 1e-5
    LOW = -3e38
    MAGIC = float(0x5F3759DF)

    x1_d = nc.dram_tensor("x1_scratch", (T, D), f32, kind="Internal").ap()

    ctx_mgr = ExitStack()
    with ctx_mgr:
        def sem(name):
            return ctx_mgr.enter_context(nc.semaphore(name))

        def persistent(name, shape, dt):
            return ctx_mgr.enter_context(nc.sbuf_tensor(name, shape, dt))

        class Region:

            def __init__(self):
                self.stack = ExitStack()

            def tensor(self, name, shape, dt):
                return self.stack.enter_context(nc.sbuf_tensor(name, shape, dt))

            def again(self):
                self.stack.close()
                self.stack = ExitStack()

        ident = persistent("ident", [P, P], f32)
        ones = persistent("ones", [P, P], f32)
        small = persistent("small", [P, 2 * KD + 2], f32)
        bq_c, bk_c = small[:, 0:KD], small[:, KD:2 * KD]
        tanh_g = persistent("tanh_g", [P, 2], f32)
        neg_mean_w = persistent("neg_mean_w", [P, KD], f32)
        row_sum_w = persistent("row_sum_w", [P, KD, 2], f32)
        bn = persistent("bn", [P, 12], f32)
        mv = persistent("mv", [P, 2], f32)
        uk = persistent("uk", [P, KD + 1], f32)
        kb_part = persistent("kb_part", [P, 1], f32)
        kb_junk = persistent("kb_junk", [P, KD], f32)
        c_cols = persistent("c_cols", [P, JB], f32)
        rs = persistent("rs", [P, 4, JB], f32)
        r1 = persistent("r1", [P, JB], f32)
        mv2 = persistent("mv2", [P, JB, 2], f32)
        ln2 = persistent("ln2", [P, 2, NT], f32)
        row_max = persistent("row_max", [P, 1], f32)
        neg_max = persistent("neg_max", [P, 2], f32)
        row_sum = persistent("row_sum", [P, 2], f32)
        att_scale = persistent("att_scale", [P, 2], f32)
        top8 = persistent("top8", [P, 16], f32)
        neg_top = persistent("neg_top", [P, 1], f32)
        gate_sum = persistent("gate_sum", [P, 2], f32)
        gate_scale = persistent("gate_scale", [P, 4], f32)
        acc_u = persistent("acc_u", [P, D], f32)
        v_bc = persistent("v_bc", [P, D], f32)

        r_m = Region()
        mt = r_m.tensor("mt", [P, 2, KD, D], f32r)
        r_1 = Region()
        wq = r_1.tensor("wq", [P, 2, KD, D], f32r)
        r_2 = Region()
        wk = r_2.tensor("wk", [P, 2, 2, H2], f32r)
        wq_raw = r_2.tensor("wq_raw", [P, 2, D], f32)
        wk_raw = r_2.tensor("wk_raw", [P, 2, H2], f32)
        r_3 = Region()
        ct = r_3.tensor("ct", [P, 2, KD, GT], f32r)
        ct_raw = r_3.tensor("ct_raw", [P, KD, GT], f32)

        r_3.again()
        bt = r_3.tensor("bt", [P, 2, KB, D], f32r)
        xn = r_3.tensor("xn", [P, D], f32)
        xnt = r_3.tensor("xnt", [P, 2, KD, P], f32r)
        x1_3 = r_3.tensor("x1_3", [P, D], f32)

        r_3.again(), r_2.again()
        cn = r_2.tensor("cn", [P, 2, D], f32r)
        at = r_2.tensor("at", [P, 2, P], f32r)
        c_bc = r_2.tensor("c_bc", [P, GT], f32)
        logits = r_2.tensor("logits", [P, 2, P], f32)
        probs = r_2.tensor("probs", [P, 2, P], f32)
        rw = r_2.tensor("rw", [RD, D], f32)
        kt = r_2.tensor("kt", [RD, NE], f32)

        r_2.again(), r_1.again()
        gbuf = r_1.tensor("gbuf", [P, KD, GT], f32)
        xt = r_1.tensor("xt", [P, KD, GT], f32)
        x_nat = r_1.tensor("x_nat", [P, JB, D], f32)
        c_nat = r_1.tensor("c_nat", [P, JB, D], f32)
        r_1.again()
        bt_raw = r_1.tensor("bt_raw", [P, KB, D], f32)
        zg = r_1.tensor("zg", [P, NB], f32)
        gate = r_1.tensor("gate", [P, NE], f32)
        sc = r_1.tensor("sc", [P, 4, NE], f32)
        zgt = r_1.tensor("zgt", [P, 2, KB, P], f32r)
        zgt_last = r_1.tensor("zgt_last", [P, 2, KB, P], f32r)

        r_1.again(), r_m.again()
        art = r_m.tensor("art", [P, 2, KD, 2, ZC], f32r)
        at_raw = r_m.tensor("at_raw", [P, KD, NB], f32)
        x1 = [r_m.tensor(f"x1_{i}", [P, D], f32) for i in range(3)] + [x1_3]
        r_m.again()

        ps = ctx_mgr.enter_context(nc.psum_tensor("ps", [P, 8, 512], f32))

        const_in, ident_in, rk_in = sem("const_in"), sem("ident_in"), sem("rk_in")
        wq_in = [[sem(f"wq_in{i}{h}") for h in range(2)] for i in range(2)]
        wk_in = [sem(f"wk_in{i}") for i in range(2)]
        ones_set, tanh_done = sem("ones_set"), sem("tanh_done")
        sum_done, mean_done, wq_hi, wq_lo = sem("sum_done"), sem("mean_done"), sem("wq_hi"), sem("wq_lo")
        wk_hi, wk_lo, wk_used = sem("wk_hi"), sem("wk_lo"), sem("wk_used")
        u_acc, v_acc = sem("u_acc"), sem("v_acc")
        mt_done, mt_hi, mt_lo = sem("mt_done"), sem("mt_hi"), sem("mt_lo")
        uv_ready, uv_done, uk_set, v_set = sem("uv_ready"), sem("uv_done"), sem("uk_set"), sem("v_set")
        ct_in = [sem(f"ct_in{i}") for i in range(2)]
        ct_hi, ct_lo, ct_pool = sem("ct_hi"), sem("ct_lo"), sem("ct_pool")
        CD, CP = 3, KD - 3
        g_done, g_set = sem("g_done"), sem("g_set")
        xt_in = sem("xt_in")
        x_in = [sem(f"x_in{i}") for i in range(JB)]
        c_in = [sem(f"c_in{i}") for i in range(JB)]
        c_done, sc_done, cb_set = sem("c_done"), sem("sc_done"), sem("cb_set")
        max_done, exp_done = sem("max_done"), sem("exp_done")
        at_done, at_hi, at_lo = sem("at_done"), sem("at_hi"), sem("at_lo")
        cn_hi, cn_lo = sem("cn_hi"), sem("cn_lo")
        att_done, x1_done, x1_stats = sem("att_done"), sem("x1_done"), sem("x1_stats")
        x1_st = [sem(f"x1_st{i}") for i in range(JB)]
        a_in = [sem(f"a_in{i}") for i in range(2)]
        b_in = [sem(f"b_in{i}") for i in range(2)]
        r_done, ar_hi, ar_lo, ar_pool, b_hi, b_lo = (
            sem(n) for n in ("r_done", "ar_hi", "ar_lo", "ar_pool", "b_hi", "b_lo"))
        POOL_A = (2, 5, 7)
        DVE_A = tuple(k for k in range(KD) if k not in POOL_A)
        x1_in = [sem(f"x1_in{i}") for i in range(4)]
        ln2_set, xn_set = sem("ln2_set"), sem("xn_set")
        xt_done, xt_hi, xt_lo = sem("xt_done"), sem("xt_hi"), sem("xt_lo")
        z_done, top_done, e_done, zg_set = sem("z_done"), sem("top_done"), sem("e_done"), sem("zg_set")
        zt_done, zt_hi, zt_lo = sem("zt_done"), sem("zt_hi"), sem("zt_lo")
        o_done, fin_set, last_o, last_fin = sem("o_done"), sem("fin_set"), sem("last_o"), sem("last_fin")
        out_st = [sem(f"out_st{i}") for i in range(4)]
        dve_self = sem("dve_self")

        block = ctx_mgr.enter_context(nc.Block())

        def wait_wk_used(eng, n):
            half, k = divmod(n, KD)
            if k == KD - 1:
                eng.wait_ge(mt_done, 8 * (half + 1))
            else:
                eng.wait_ge(wk_used, n - half + 1)

        def f(ap):
            return ap.bitcast(f32)

        @block.sync
        def _(sp):
            def load_wk(n):
                if n >= 2:
                    sp.wait_ge(wk_lo, n - 1)
                    sp.wait_ge(v_acc, n - 1)
                half, k = divmod(n, KD)
                sp.dma_start(wk_raw[:, n % 2, :], wk_d[k * P:(k + 1) * P, half * H2:(half + 1) * H2])\
                    .then_inc(wk_in[n % 2], 16)

            for k in range(KD):
                if k >= 2:
                    sp.wait_ge(wq_lo, 2 * (k - 1))
                    sp.wait_ge(u_acc, k - 1)
                for h in range(2):
                    cols = slice(h * H2, (h + 1) * H2)
                    sp.dma_start(wq_raw[:, k % 2, cols], wq_d[k * P:(k + 1) * P, cols])\
                        .then_inc(wq_in[k % 2][h], 16)
                if k > 0:
                    load_wk(k)
                else:
                    sp.dma_start(ident[:], ident_d).then_inc(ident_in, 16)

            def load_ct(g, h):
                sp.dma_start(ct_raw[:, h * 4:(h + 1) * 4, :],
                             ctx_t[h * H2:(h + 1) * H2, bass.ds(g * GT, GT)].rearrange("(k p) t -> p k t", p=P))\
                    .then_inc(ct_in[h], 16)

            load_ct(0, 0)
            sp.wait_ge(sum_done, 2 * KD)
            load_ct(0, 1)
            for n in range(KD, 2 * KD):
                load_wk(n)
            sp.wait_ge(mt_done, 16)

            def load_xt(g):
                sp.dma_start(xt[:], x_t[:, bass.ds(g * GT, GT)].rearrange("(k p) t -> p k t", p=P))\
                    .then_inc(xt_in, 16)

            def load_c(g, j):
                sp.dma_start(c_nat[:, j, :], ctx[bass.ds(g * GT + j * P, P), :]).then_inc(c_in[j], 16)

            def load_x(g, j):
                sp.dma_start(x_nat[:, j, :], x[bass.ds(g * GT + j * P, P), :]).then_inc(x_in[j], 16)

            for j in range(JB):
                load_c(0, j)
            load_xt(0)
            sp.wait_ge(v_acc, 2 * KD)
            sp.dma_start(rw[:], router_w).then_inc(rk_in, 16)
            sp.dma_start(kt[:], keys_t).then_inc(rk_in, 16)
            for h in range(2):
                sp.wait_ge(ct_pool, (KD // 2, CP)[h])
                if h == 1:
                    sp.wait_ge(ct_lo, CD)
                load_ct(1, h)
            for j in range(JB):
                load_x(0, j)

            def group(g, more_ct, between=None):
                if more_ct:
                    for h in range(2):
                        sp.wait_ge(ct_pool, g * CP + (CP + (KD // 2, CP)[h]))
                        if h == 1:
                            sp.wait_ge(ct_lo, g * CD + 2 * CD)
                        load_ct(g + 2, h)
                sp.wait_ge(sc_done, g * JB + JB)
                load_xt(g + 1)
                for j in range(JB):
                    if j >= 1:
                        sp.wait_ge(x1_st[j - 1], g * 16 + 16)
                        sp.wait_ge(x1_stats, g * JB + j)
                        load_x(g + 1, j - 1)
                    sp.wait_ge(cn_lo, g * JB + (j + 1))
                    load_c(g + 1, j)
                    if between and j == JB - 1:
                        between()
                    sp.wait_ge(x1_done, g * JB + (j + 1))
                    sp.dma_start(x1_d[bass.ds(g * GT + j * P, P), :], x_nat[:, j, :]).then_inc(x1_st[j], 16)
                sp.wait_ge(x1_st[JB - 1], g * 16 + 16)
                sp.wait_ge(x1_stats, g * JB + JB)
                load_x(g + 1, JB - 1)

            def load_x1(t, slot):
                sp.dma_start(x1[slot][:], x1_d[bass.ds(t * P, P), :]).then_inc(x1_in[slot], 16)

            def load_first_weights():
                sp.wait_ge(g_done, NG * KD)
                for h in range(2):
                    load_x1(h, h)
                    sp.dma_start(at_raw[:, 4 * h:4 * h + 4, :],
                                 a_t[h * H2:(h + 1) * H2, :].rearrange("(k p) n -> p k n", p=P))\
                        .then_inc(a_in[h], 16)

            with sp.Fori(0, NG - 2) as g:
                group(g, True)
            group(NG - 2, False, load_first_weights)
            sp.wait_ge(sc_done, NT)
            for h in range(2):
                sp.dma_start(bt_raw[:, h * (KB // 2):(h + 1) * (KB // 2), :],
                             b_t[h * (NB // 2):(h + 1) * (NB // 2), :].rearrange("(k p) n -> p k n", p=P))\
                    .then_inc(b_in[h], 16)
            load_x1(2, 2)
            load_x1(3, 3)

            def store_out(t, u):
                sp.wait_ge(fin_set, t + 1)
                sp.dma_start(out[bass.ds(t * P, P), :], x1[u][:]).then_inc(out_st[u], 16)

            def next_tile(t, u, n):
                sp.wait_ge(out_st[u], n)
                load_x1(t + 4, u)

            for j in range(JB):
                sp.wait_ge(x1_done, (NG - 1) * JB + j + 1)
                sp.dma_start(x1_d[(NG - 1) * GT + j * P:(NG - 1) * GT + (j + 1) * P, :], x_nat[:, j, :])\
                    .then_inc(x1_st[j], 16)
                store_out(j, j)
                next_tile(j, j, 16)
            for j in range(JB):
                sp.wait_ge(x1_st[j], 16 * NG)
            with sp.Fori(0, 2) as i:
                for w in range(4):
                    store_out(i * 4 + (w + 4), w)
                    next_tile(i * 4 + (w + 4), w, i * 16 + 32)
            for t in range(NT - 4, NT - 1):
                store_out(t, t % 4)
            for h in range(2):
                sp.wait_ge(last_fin, h + 1)
                cols = slice(h * H2, (h + 1) * H2)
                sp.dma_start(out[(NT - 1) * P:NT * P, cols], x1[3][:, cols]).then_inc(out_st[3], 16)
            for u in range(4):
                sp.wait_ge(out_st[u], 16 * (NT // 4 + (u == 3)))

        @block.gpsimd
        def _(pool):
            pool.memset(ones[:], 1.0).then_inc(ones_set, 1)

            def split_ct(g, k):
                pool.wait_ge(ct_hi, g * KD + (k + 1))
                nc.gpsimd.tensor_tensor(ct[:, 1, k, :], ct_raw[:, k, :], f(ct[:, 0, k, :]), ALU.subtract)\
                    .then_inc(ct_pool, 1)

            for n in range(2 * KD):
                pool.wait_ge(wk_hi, n + 1)
                nc.gpsimd.tensor_tensor(wk[:, n % 2, 1, :], wk_raw[:, n % 2, :], f(wk[:, n % 2, 0, :]),
                                        ALU.subtract).then_inc(wk_lo, 1)
                if 0 <= n - (KD + 2) < CP:
                    split_ct(0, n - (KD + 2))

            def split_c(g, j):
                pool.wait_ge(cn_hi, g * JB + (j + 1))
                nc.gpsimd.tensor_tensor(cn[:, 1, :], c_nat[:, j, :], f(cn[:, 0, :]), ALU.subtract)\
                    .then_inc(cn_lo, 1)

            with pool.Fori(0, NG - 1) as g:
                for k in range(CP):
                    split_ct(g + 1, k)
                for j in range(JB):
                    split_c(g, j)
            for k in POOL_A:
                pool.wait_ge(ar_hi, k + 2)
                nc.gpsimd.tensor_tensor(art[:, 1, k, :, 0:NB // 2],
                                        at_raw[:, k, :].rearrange("p (c n) -> p c n", c=2),
                                        f(art[:, 0, k, :, 0:NB // 2]), ALU.subtract).then_inc(ar_pool, 1)
            split_c(NG - 1, 0)
            for k in range(KB):
                pool.wait_ge(b_hi, k + 1)
                nc.gpsimd.tensor_tensor(bt[:, 1, k, :], bt_raw[:, k, :], f(bt[:, 0, k, :]), ALU.subtract)\
                    .then_inc(b_lo, 1)
            for j in range(1, JB):
                split_c(NG - 1, j)

        @block.scalar
        def _(act):
            act.dma_start(small[:], smalls).then_inc(const_in, 16)
            act.dma_start(wk_raw[:, 0, :], wk_d[0:P, 0:H2]).then_inc(wk_in[0], 16)
            act.wait_ge(const_in, 16)
            nc.scalar.activation(tanh_g[:], small[:, 2 * KD:2 * KD + 2], ACT.Tanh).then_inc(tanh_done, 1)

            def split_wk(n):
                act.wait_ge(wk_in[n % 2], 16 * (n // 2 + 1))
                if n >= 2:
                    wait_wk_used(act, n - 2)
                nc.scalar.activation(wk[:, n % 2, 0, :], wk_raw[:, n % 2, :], ACT.Copy).then_inc(wk_hi, 1)

            def evac_mt(p, b):
                act.wait_ge(mt_done, 8 * p + b + 1)
                nc.scalar.activation(mt[:, 0, 4 * p + b % 4, (b // 4) * H2:(b // 4 + 1) * H2], ps[:, b, :],
                                     ACT.Copy).then_inc(mt_hi, 1)

            def sum_wq(k):
                for h in range(2):
                    cols = slice(h * H2, (h + 1) * H2)
                    act.wait_ge(wq_in[k % 2][h], 16 * (k // 2 + 1))
                    n = 2 * k + h
                    if n >= 4:
                        act.wait_ge(sum_done, n - 3)
                    nc.scalar.activation(ct_raw[:, KD // 2 + n % 4, :], wq_raw[:, k % 2, cols], ACT.Copy,
                                         accum_out=row_sum_w[:, k, h:h + 1]).then_inc(sum_done, 1)

            for k in range(KD):
                sum_wq(k)
                split_wk(k)
                act.wait_ge(mean_done, k + 1)
                for h in range(2):
                    cols = slice(h * H2, (h + 1) * H2)
                    nc.scalar.activation(wq[:, 0, k, cols], wq_raw[:, k % 2, cols], ACT.Identity,
                                         bias=neg_mean_w[:, k:k + 1]).then_inc(wq_hi, 1)
            split_wk(KD)
            for b in range(8):
                evac_mt(0, b)
                if b == 3:
                    split_wk(KD + 1)

            def split_ct(g, k):
                act.wait_ge(ct_in[k // 4], g * 16 + 16)
                nc.scalar.activation(ct[:, 0, k, :], ct_raw[:, k, :], ACT.Copy).then_inc(ct_hi, 1)

            for n in range(KD + 2, 2 * KD):
                split_wk(n)
                split_ct(0, n - (KD + 2))
            for k in (KD - 2, KD - 1):
                split_ct(0, k)
            for b in range(8):
                evac_mt(1, b)

            def evac_g(g, i):
                act.wait_ge(g_done, g * KD + (i + 1))
                nc.scalar.activation(gbuf[:, i, :], ps[:, i % 2, :], ACT.Identity, bias=uk[:, i:i + 1])\
                    .then_inc(g_set, 1)

            act.wait_ge(uv_done, 1)
            nc.scalar.activation(uk[:], ps[:, 2, 0:KD + 1], ACT.Copy).then_inc(uk_set, 1)
            act.wait_ge(uk_set, 1)
            for i in range(KD):
                evac_g(0, i)

            def exp(g, j):
                act.wait_ge(max_done, g * JB + (j + 1))
                nc.scalar.activation(probs[:, j % 2, :], logits[:, j % 2, :], ACT.Exp,
                                     bias=neg_max[:, j % 2:j % 2 + 1], scale=SCALE,
                                     accum_out=row_sum[:, j % 2:j % 2 + 1]).then_inc(exp_done, 1)

            def split_at(g, j):
                act.wait_ge(at_done, g * JB + (j + 1))
                nc.scalar.activation(at[:, 0, :], ps[:, 7, j * P:(j + 1) * P], ACT.Copy).then_inc(at_hi, 1)

            def split_c(g, j):
                act.wait_ge(c_in[j], g * 16 + 16)
                if j > 0:
                    act.wait_ge(att_done, g * JB + j)
                nc.scalar.activation(cn[:, 0, :], c_nat[:, j, :], ACT.Copy).then_inc(cn_hi, 1)

            def evac_c(g):
                act.wait_ge(sc_done, g * JB + JB)
                nc.scalar.activation(c_bc[:], ps[:, 4, :], ACT.Identity, bias=uk[:, KD:KD + 1]).then_inc(cb_set, 1)

            with act.Fori(0, NG - 1) as g:
                act.wait_ge(g_done, g * KD + KD)
                for k in range(KD):
                    split_ct(g + 1, k)
                evac_c(g)
                split_c(g, 0)
                exp(g, 0)
                for j in range(JB):
                    evac_g(g + 1, 2 * j)
                    split_at(g, j)
                    if j + 1 < JB:
                        exp(g, j + 1)
                    evac_g(g + 1, 2 * j + 1)
                    if j + 1 < JB:
                        split_c(g, j + 1)

            def split_a(k):
                act.wait_ge(a_in[k // 4], 16)
                nc.scalar.activation(art[:, 0, k, :, 0:NB // 2], at_raw[:, k, :].rearrange("p (c n) -> p c n", c=2),
                                     ACT.Copy).then_inc(ar_hi, 1)

            def split_b(k):
                act.wait_ge(b_in[k // (KB // 2)], 16)
                nc.scalar.activation(bt[:, 0, k, :], bt_raw[:, k, :], ACT.Copy).then_inc(b_hi, 1)

            def normalize(t, u, n):
                act.wait_ge(x1_in[u], n)
                nc.scalar.activation(xn[:], x1[u][:], ACT.Identity, bias=ln2[:, 1, bass.ds(t, 1)],
                                     scale=ln2[:, 0, bass.ds(t, 1)]).then_inc(xn_set, 1)

            def split_xt(s, halves=(0, 1)):
                for h in halves:
                    act.wait_ge(xt_done, s * 2 + (h + 1))
                    nc.scalar.activation(xnt[:, 0, 4 * h:4 * h + 4, :].rearrange("p k t -> p (k t)"),
                                         ps[:, 2 + h, :], ACT.Copy).then_inc(xt_hi, 1)

            def split_zt(s, to=zgt):
                act.wait_ge(zt_done, s + 1)
                nc.scalar.activation(to[:, 0, :, :].rearrange("p k t -> p (k t)"), ps[:, 4, :], ACT.Copy)\
                    .then_inc(zt_hi, 1)

            def exp_top(s):
                act.wait_ge(top_done, s + 1)
                nc.scalar.activation(sc[:, 3, :], sc[:, 0, :], ACT.Exp, bias=neg_top[:]).then_inc(e_done, 1)

            last_g = NG - 1
            act.wait_ge(r_done, 1)
            nc.scalar.activation(art[:, 0, :, :, NB // 2:ZC],
                                 ps[:, 1, :].rearrange("p (k c e) -> p k c e", k=KD, c=2), ACT.Copy)\
                .then_inc(ar_hi, 1)
            act.wait_ge(ln2_set, 1)
            normalize(0, 0, 16)
            for k in range(KD):
                if k == KD // 2 - 1:
                    split_xt(0)
                    normalize(1, 1, 16)
                if k == KD - 1:
                    evac_c(last_g)
                split_a(k)
            split_xt(1, (0,))
            split_c(last_g, 0)
            exp(last_g, 0)
            split_xt(1, (1,))
            split_at(last_g, 0)
            for k in range(KB):
                if k == KB // 2:
                    exp_top(0)
                split_b(k)
            for s in range(1, JB + 1):
                j = s - 1
                if s == 1:
                    normalize(2, 2, 16)
                else:
                    split_at(last_g, j)
                split_zt(s - 1)
                if j + 1 < JB:
                    exp(last_g, j + 1)
                if s + 1 == JB:
                    act.wait_ge(ln2_set, 2)
                if s > 1:
                    normalize(s + 1, (s + 1) % 4, 16 * ((s + 1) // 4 + 1))
                if j + 1 < JB:
                    split_c(last_g, j + 1)
                exp_top(s)
                split_xt(s + 1)

            def tile(s, u, n):
                split_zt(s - 1)
                normalize(s + 1, u, n)
                exp_top(s)
                split_xt(s + 1)

            with act.Fori(0, 2) as i:
                for w in range(4):
                    if w == 2:
                        act.wait_ge(ln2_set, i + 3)
                    tile(i * 4 + (w + 5), (w + 2) % 4, i * 16 + 16 * ((w + 6) // 4 + 1))
            for s in range(NT - 3, NT - 1):
                tile(s, (s + 1) % 4, 16 * ((s + 1) // 4 + 1))
            split_zt(NT - 2)
            exp_top(NT - 1)
            split_zt(NT - 1, zgt_last)

        @block.vector
        def _(dve):
            own = SelfSync(dve, dve_self)

            def tt(out_, a, b, op):
                return nc.vector.tensor_tensor(out_, a, b, op)

            def row_stats(src, to=mv[:]):
                nc.vector.bn_stats(bn[:, 0:6], src[:, 0:H2])
                own.done(nc.vector.bn_stats(bn[:, 6:12], src[:, H2:D]))
                return nc.vector.bn_aggr(to, bn[:])

            def rstd_of(var, w):
                y, v, h, a = (rs[:, c, 0:w] for c in range(4))
                nc.vector.tensor_scalar(h, var, -0.5, -0.5 * EPS, ALU.mult, ALU.add)
                own.done(nc.vector.tensor_scalar(v, var, EPS, None, ALU.add))
                own.done(nc.vector.tensor_scalar(a.bitcast(i32), v.bitcast(i32), 1, None, ALU.logical_shift_right))
                own.done(nc.vector.tensor_scalar(y.bitcast(i32), a.bitcast(i32), -1.0, MAGIC, ALU.mult, ALU.add))
                for step in range(3):
                    if w == 1:
                        own.done(nc.vector.scalar_tensor_tensor(a, y, h, y, ALU.mult, ALU.mult))
                    else:
                        own.done(tt(a, y, y, ALU.mult))
                        own.done(tt(a, a, h, ALU.mult))
                    own.done(nc.vector.scalar_tensor_tensor(y, a, 1.5, y, ALU.add, ALU.mult))

            def add_to_v(n):
                half, k = divmod(n, KD)
                dve.wait_ge(wk_in[n % 2], 16 * (n // 2 + 1))
                if n > 0:
                    dve.wait_ge(v_acc, n)
                vh = v_bc[:, half * H2:(half + 1) * H2]
                raw = wk_raw[:, n % 2, :]
                if k == 0:
                    nc.vector.tensor_scalar(vh, raw, bq_c[:, 0:1], None, ALU.mult).then_inc(v_acc, 1)
                else:
                    nc.vector.scalar_tensor_tensor(vh, raw, bq_c[:, k:k + 1], vh, ALU.mult, ALU.add)\
                        .then_inc(v_acc, 1)

            def evac_mt(p, b):
                dve.wait_ge(mt_hi, 8 * p + b + 1)
                cols = slice((b // 4) * H2, (b // 4 + 1) * H2)
                tt(mt[:, 1, 4 * p + b % 4, cols], ps[:, b, :], f(mt[:, 0, 4 * p + b % 4, cols]), ALU.subtract)\
                    .then_inc(mt_lo, 1)

            for k in range(KD):
                raw = wq_raw[:, k % 2, :]
                dve.wait_ge(sum_done, 2 * k + 2)
                own.done(tt(mv[:, 0:1], row_sum_w[:, k, 0:1], row_sum_w[:, k, 1:2], ALU.add))
                nc.vector.tensor_scalar(neg_mean_w[:, k:k + 1], mv[:, 0:1], -1.0 / D, None, ALU.mult)\
                    .then_inc(mean_done, 1)
                dve.wait_ge(const_in, 16)
                add_to_v(k)
                for h in range(2):
                    dve.wait_ge(wq_hi, 2 * k + h + 1)
                    cols = slice(h * H2, (h + 1) * H2)
                    nc.vector.scalar_tensor_tensor(wq[:, 1, k, cols], raw[:, cols], neg_mean_w[:, k:k + 1],
                                                   f(wq[:, 0, k, cols]), ALU.add, ALU.subtract).then_inc(wq_lo, 1)
                if k == 0:
                    nc.vector.tensor_scalar(acc_u[:], raw, bk_c[:, 0:1], None, ALU.mult).then_inc(u_acc, 1)
                else:
                    nc.vector.scalar_tensor_tensor(acc_u[:], raw, bk_c[:, k:k + 1], acc_u[:],
                                                   ALU.mult, ALU.add).then_inc(u_acc, 1)
                dve.wait_ge(u_acc, k + 1)
            own.done(nc.vector.tensor_tensor(kb_junk[:], bq_c, bk_c, ALU.mult))
            own.done(nc.vector.tensor_reduce(kb_part[:], kb_junk[:], AX.X, ALU.add))
            own.done(row_stats(acc_u))
            own.done(nc.vector.tensor_scalar(acc_u[:], acc_u[:], mv[:, 0:1], None, ALU.subtract))
            add_to_v(KD)
            for b in range(8):
                evac_mt(0, b)
                if b == 3:
                    add_to_v(KD + 1)

            def split_ct(g, k):
                dve.wait_ge(ct_hi, g * KD + (k + 1))
                tt(ct[:, 1, k, :], ct_raw[:, k, :], f(ct[:, 0, k, :]), ALU.subtract).then_inc(ct_lo, 1)

            for n in range(KD + 2, 2 * KD):
                add_to_v(n)
                if n - (KD + 2) >= CP:
                    split_ct(0, n - (KD + 2))
            for k in (KD - 2, KD - 1):
                split_ct(0, k)
            dve.wait_ge(v_acc, 2 * KD)
            nc.vector.tensor_copy(kb_junk[:, 0:1], kb_part[:]).then_inc(uv_ready, 1)
            for b in range(8):
                evac_mt(1, b)
            dve.wait_ge(uv_done, 1)
            own.done(nc.vector.tensor_copy(v_bc[:].rearrange("p (h n) -> p h n", h=2), ps[:, 5:7, :]))

            def c_column(g, j):
                dve.wait_ge(c_in[j], g * 16 + 16)
                if not (isinstance(g, int) and g == 0 and j == 0):
                    dve.wait_ge(c_done, g * JB + j)
                nc.vector.scalar_tensor_tensor(acc_u[:], c_nat[:, j, :], 1.0, v_bc[:], ALU.mult, ALU.mult,
                                               accum_out=c_cols[:, j:j + 1]).then_inc(c_done, 1)

            for j in range(JB):
                c_column(0, j)

            def stats1(g, j):
                dve.wait_ge(x_in[j], g * 16 + 16)
                own.done(row_stats(x_nat[:, j, :]))

            def rstd1(j):
                rstd_of(mv[:, 1:2], 1)
                own.done(nc.vector.tensor_copy(r1[:, j:j + 1], rs[:, 0, 0:1]))

            def norm1(g, j):
                stats1(g, j)
                rstd1(j)

            def softmax_head(g, j):
                if j == 0:
                    dve.wait_ge(cb_set, g + 1)
                if j >= 2:
                    dve.wait_ge(exp_done, g * JB + (j - 1))
                own.done(nc.vector.scalar_tensor_tensor(
                    logits[:, j % 2, :], ps[:, 7, j * P:(j + 1) * P], r1[:, j:j + 1],
                    c_bc[:, j * P:(j + 1) * P], ALU.mult, ALU.add))
                own.done(nc.vector.tensor_reduce(row_max[:], logits[:, j % 2, :], AX.X, ALU.max))
                nc.vector.tensor_scalar(neg_max[:, j % 2:j % 2 + 1], row_max[:], -SCALE, None, ALU.mult)\
                    .then_inc(max_done, 1)

            def split_at(g, j):
                dve.wait_ge(at_hi, g * JB + (j + 1))
                tt(at[:, 1, :], ps[:, 7, j * P:(j + 1) * P], f(at[:, 0, :]), ALU.subtract).then_inc(at_lo, 1)
                own.done(nc.vector.reciprocal(att_scale[:, 0:1], row_sum[:, j % 2:j % 2 + 1]))
                own.done(tt(att_scale[:, 1:2], att_scale[:, 0:1], tanh_g[:, 0:1], ALU.mult))

            def add_attended(g, j, bank):
                dve.wait_ge(att_done, g * JB + (j + 1))
                xj = x_nat[:, j, :].rearrange("p (h n) -> p h n", h=2)
                nc.vector.scalar_tensor_tensor(xj, ps[:, bank:bank + 2, :], att_scale[:, 1:2], xj,
                                               ALU.mult, ALU.add).then_inc(x1_done, 1)

            def stats2(g, j):
                dve.wait_ge(x1_done, g * JB + (j + 1))
                row_stats(x_nat[:, j, :], mv2[:, j, :]).then_inc(x1_stats, 1)
                dve.wait_ge(x1_stats, g * JB + (j + 1))

            def norm2(g, j, n):
                rstd_of(mv2[:, j:j + n, 1], n)
                own.done(nc.vector.tensor_copy(ln2[:, 0, bass.ds(g * JB + j, n)], rs[:, 0, 0:n]))
                last = nc.vector.scalar_tensor_tensor(ln2[:, 1, bass.ds(g * JB + j, n)], mv2[:, j:j + n, 0], -1.0,
                                                      rs[:, 0, 0:n], ALU.mult, ALU.mult)
                if j + n == JB:
                    last.then_inc(ln2_set, 1)
                    dve.wait_ge(ln2_set, g + 1)
                else:
                    own.done(last)

            dve.wait_ge(tanh_done, 1)
            for j in range(2):
                norm1(0, j)
            with dve.Fori(0, NG - 1) as g:
                own.restart()
                for k in range(CP, KD):
                    split_ct(g + 1, k)
                softmax_head(g, 0)
                for j in range(JB):
                    if j == JB - 1:
                        norm2(g, 0, JB - 1)
                    if j >= 1:
                        c_column(g + 1, j - 1)
                    split_at(g, j)
                    if j + 1 < JB:
                        softmax_head(g, j + 1)
                    if j < 2:
                        norm1(g, j + 2)
                    else:
                        norm1(g + 1, j - 2)
                    if j == JB - 1:
                        c_column(g + 1, j)
                    add_attended(g, j, 5)
                    stats2(g, j)
                norm2(g, JB - 1, 1)
            own.restart()

            def split_a(k):
                dve.wait_ge(ar_hi, k + 2)
                tt(art[:, 1, k, :, 0:NB // 2], at_raw[:, k, :].rearrange("p (c n) -> p c n", c=2),
                   f(art[:, 0, k, :, 0:NB // 2]), ALU.subtract).then_inc(ar_lo, 1)

            def split_xt(s, halves=(0, 1)):
                for h in halves:
                    dve.wait_ge(xt_hi, s * 2 + (h + 1))
                    tt(xnt[:, 1, 4 * h:4 * h + 4, :].rearrange("p k t -> p (k t)"), ps[:, 2 + h, :],
                       f(xnt[:, 0, 4 * h:4 * h + 4, :]).rearrange("p k t -> p (k t)"), ALU.subtract)\
                        .then_inc(xt_lo, 1)

            def split_zt(s, to=zgt):
                dve.wait_ge(zt_hi, s + 1)
                tt(to[:, 1, :, :].rearrange("p k t -> p (k t)"), ps[:, 4, :],
                   f(to[:, 0, :, :]).rearrange("p k t -> p (k t)"), ALU.subtract).then_inc(zt_lo, 1)

            def gates(s, u, bank=0):
                dve.wait_ge(z_done, s + 1)
                own.done(nc.vector.tensor_copy(sc[:, 0, :].rearrange("p (c e) -> p c e", c=2),
                                               ps[:, bank:bank + 2, NB // 2:ZC]))
                own.done(nc.vector.max(top8[:, 0:8], sc[:, 0, :]))
                nc.vector.tensor_scalar(neg_top[:], top8[:, 0:1], -1.0, None, ALU.mult).then_inc(top_done, 1)
                own.done(nc.vector.match_replace(sc[:, 1, :], top8[:, 0:8], sc[:, 0, :], LOW))
                own.done(nc.vector.max(top8[:, 8:16], sc[:, 1, :]))
                own.done(nc.vector.match_replace(sc[:, 2, :], top8[:, 8:16], sc[:, 1, :], LOW))
                dve.wait_ge(e_done, s + 1)
                own.done(nc.vector.scalar_tensor_tensor(gate[:], sc[:, 2, :], LOW, sc[:, 3, :], ALU.is_equal,
                                                        ALU.mult, accum_out=gate_sum[:, 0:1]))
                nc.vector.tensor_tensor(
                    zg[:].rearrange("p (c e r) -> p c e r", c=2, r=RANK),
                    ps[:, bank:bank + 2, 0:NB // 2].rearrange("p c (e r) -> p c e r", r=RANK),
                    gate[:].rearrange("p (c e) -> p c e", c=2).unsqueeze(3).to_broadcast([P, 2, NE // 2, RANK]),
                    ALU.mult).then_inc(zg_set, 1)
                own.done(nc.vector.reciprocal(gate_sum[:, 1:2], gate_sum[:, 0:1]))
                own.done(nc.vector.scalar_tensor_tensor(gate_scale[:, u:u + 1], gate_sum[:, 1:2], SCALING,
                                                        tanh_g[:, 1:2], ALU.mult, ALU.mult))

            def finish(s, u):
                dve.wait_ge(o_done, s + 1)
                xu = x1[u][:].rearrange("p (h n) -> p h n", h=2)
                nc.vector.scalar_tensor_tensor(xu, ps[:, 5:7, :], gate_scale[:, u:u + 1], xu, ALU.mult, ALU.add)\
                    .then_inc(fin_set, 1)

            last_g = NG - 1
            dve.wait_ge(ar_hi, 1)
            tt(art[:, 1, :, :, NB // 2:ZC], ps[:, 1, :].rearrange("p (k c e) -> p k c e", k=KD, c=2),
               f(art[:, 0, :, :, NB // 2:ZC]), ALU.subtract).then_inc(ar_lo, 1)
            for k in DVE_A:
                if k == DVE_A[2]:
                    split_xt(0)
                split_a(k)
            softmax_head(last_g, 0)
            split_xt(1, (0,))
            norm1(last_g, JB - 2)
            split_xt(1, (1,))
            split_at(last_g, 0)
            gates(0, 0, 5)
            for s in range(1, JB + 1):
                j = s - 1
                if s == 1:
                    add_attended(last_g, j, 2)
                    split_zt(s - 1)
                    softmax_head(last_g, j + 1)
                else:
                    split_at(last_g, j)
                    split_zt(s - 1)
                    if j + 1 < JB:
                        softmax_head(last_g, j + 1)
                    add_attended(last_g, j, 2)
                    if s == 2:
                        stats1(last_g, JB - 1)
                stats2(last_g, j)
                gates(s, s % 4)
                if s == 2:
                    rstd1(JB - 1)
                split_xt(s + 1)
                finish(s - 1, (s - 1) % 4)
            norm2(last_g, 0, JB)

            def tile(s, u):
                split_zt(s - 1)
                gates(s, u)
                split_xt(s + 1)
                finish(s - 1, (u - 1) % 4)

            with dve.Fori(0, 2) as i:
                own.restart()
                for w in range(4):
                    tile(i * 4 + (w + 5), (w + 1) % 4)
            own.restart()
            for s in range(NT - 3, NT - 1):
                tile(s, s % 4)
            split_zt(NT - 2)
            gates(NT - 1, 3)
            split_zt(NT - 1, zgt_last)
            finish(NT - 2, 2)
            for h in range(2):
                dve.wait_ge(last_o, h + 1)
                cols = slice(h * H2, (h + 1) * H2)
                nc.vector.scalar_tensor_tensor(x1[3][:, cols], ps[:, 2 + h, :], gate_scale[:, 3:4], x1[3][:, cols],
                                               ALU.mult, ALU.add).then_inc(last_fin, 1)

        @block.tensor
        def _(pe):
            HILO = ((0, 0), (0, 1), (1, 0))

            pe.wait_ge(ones_set, 1)
            for _ in range(12):
                nc.tensor.matmul(ps[:, 7, 0:P], ones[:], ones[:], start=True, stop=True)
            for p in range(2):
                for k in range(KD):
                    n = p * KD + k
                    order = [(b, q) for b in range(8) for q in range(3)]
                    if n < 2:
                        order.sort(key=lambda bq: bq[1])
                    for i, (b, q) in enumerate(order):
                        h, j = divmod(b, 4)
                        a, c = HILO[q]
                        if i == 0:
                            pe.wait_ge(wk_hi, n + 1)
                        if n < 2 and (b, q) == (0, 2) or n >= 2 and i == 0:
                            pe.wait_ge(wk_lo, n + 1)
                        if p == 0 and j == 0 and q == 0:
                            pe.wait_ge(wq_hi, 2 * k + h + 1)
                        if p == 0 and j == 0 and q == 1:
                            pe.wait_ge(wq_lo, 2 * k + h + 1)
                        if p == 1 and k == 0 and q == 0:
                            pe.wait_ge(mt_lo, b + 1)
                        last = nc.tensor.matmul(ps[:, b, :], wk[:, n % 2, a, j * P:(j + 1) * P],
                                                wq[:, c, k, h * H2:(h + 1) * H2],
                                                start=(k == 0 and q == 0), stop=(k == KD - 1 and q == 2))
                        if k == KD - 1 and q == 2:
                            last.then_inc(mt_done, 1)
                    if k < KD - 1:
                        last.then_inc(wk_used, 1)

            def g_chunk(g, i):
                if not isinstance(g, int) or g > 0:
                    pe.wait_ge(g_set, g * KD + (i - 1))
                elif i >= 2:
                    pe.wait_ge(g_set, i - 1)
                else:
                    pe.wait_ge(mt_lo, 8 + i + 1)
                for k in range(KD):
                    if i == 0:
                        if k < CP:
                            pe.wait_ge(ct_pool, g * CP + (k + 1))
                        else:
                            pe.wait_ge(ct_lo, g * CD + (k - CP + 1))
                        if isinstance(g, int) and g == 0 and k >= 4:
                            pe.wait_ge(mt_lo, 8 + (k - 4) + 1)
                    for q, (a, c) in enumerate(HILO):
                        last = nc.tensor.matmul(ps[:, i % 2, :], mt[:, a, k, i * P:(i + 1) * P], ct[:, c, k, :],
                                                start=(k == 0 and q == 0), stop=(k == KD - 1 and q == 2))
                last.then_inc(g_done, 1)

            g_chunk(0, 0)
            pe.wait_ge(uv_ready, 1)
            pe.wait_ge(ones_set, 1)
            pe.wait_ge(mt_lo, 16)
            for i in range(KD):
                nc.tensor.matmul(ps[:, 2, i:i + 1], acc_u[:, i * P:(i + 1) * P], ones[:, 0:1], start=True, stop=True)
            nc.tensor.matmul(ps[:, 2, KD:KD + 1], ones[:], kb_part[:], start=True, stop=True)
            for h in range(2):
                last = nc.tensor.matmul(ps[:, 5 + h, :], ones[:], v_bc[:, h * H2:(h + 1) * H2], start=True, stop=True)
            last.then_inc(uv_done, 1)
            for i in range(1, KD):
                g_chunk(0, i)

            pe.wait_ge(ident_in, 16)

            def scores(g, js=range(JB)):
                if js[0] == 0:
                    pe.wait_ge(xt_in, g * 16 + 16)
                    pe.wait_ge(g_set, g * KD + (KD - 1))
                for j in js:
                    cols = slice(j * P, (j + 1) * P)
                    for k in range(KD):
                        if j == 0 and k == KD - 1:
                            pe.wait_ge(g_set, g * KD + KD)
                        nc.tensor.matmul(ps[:, 7, cols], xt[:, k, cols], gbuf[:, k, cols],
                                         start=(k == 0), stop=(k == KD - 1))
                    pe.wait_ge(c_done, g * JB + (j + 1))
                    nc.tensor.transpose(ps[:, 4, cols], c_cols[:, j:j + 1].to_broadcast([P, P]), ident[:])\
                        .then_inc(sc_done, 1)

            def transpose_probs(g, j):
                pe.wait_ge(exp_done, g * JB + (j + 1))
                nc.tensor.transpose(ps[:, 7, j * P:(j + 1) * P], probs[:, j % 2, :], ident[:]).then_inc(at_done, 1)

            def attend(g, j, bank):
                pe.wait_ge(at_lo, g * JB + (j + 1))
                pe.wait_ge(cn_lo, g * JB + (j + 1))
                for h in range(2):
                    for q, (a, c) in enumerate(HILO):
                        last = nc.tensor.matmul(ps[:, bank + h, :], at[:, a, :], cn[:, c, h * H2:(h + 1) * H2],
                                                start=(q == 0), stop=(q == 2))
                last.then_inc(att_done, 1)

            with pe.Fori(0, NG - 1) as g:
                scores(g)
                g_chunk(g + 1, 0)
                for j in range(JB):
                    transpose_probs(g, j)
                    g_chunk(g + 1, 2 * j + 1)
                    if j > 0:
                        pe.wait_ge(x1_done, g * JB + j)
                    attend(g, j, 5)
                    if j + 1 < JB:
                        g_chunk(g + 1, 2 * j + 2)
            pe.wait_ge(rk_in, 32)
            pe.wait_ge(g_set, NG * KD)
            for k in range(KD):
                last = nc.tensor.matmul(ps[:, 1, k * NE:(k + 1) * NE], rw[:, k * P:(k + 1) * P], kt[:],
                                        start=True, stop=True)
            last.then_inc(r_done, 1)

            def transpose_x(s, halves=(0, 1)):
                pe.wait_ge(xn_set, s + 1)
                for h in halves:
                    for k in range(4):
                        c = 4 * h + k
                        last = nc.tensor.transpose(ps[:, 2 + h, k * P:(k + 1) * P], xn[:, c * P:(c + 1) * P],
                                                   ident[:])
                    last.then_inc(xt_done, 1)

            def experts_in(s, halves=(0, 1), first=False, bank=0):
                for half in halves:
                    for q, (a, c) in enumerate(HILO):
                        if q == 0:
                            pe.wait_ge(xt_hi, s * 2 + (half + 1))
                        if q == 2:
                            pe.wait_ge(xt_lo, s * 2 + (half + 1))
                        for k in range(half * KD // 2, (half + 1) * KD // 2):
                            if first and q == 0:
                                pe.wait_ge(ar_hi, k + 2)
                            if first and q == 1:
                                if k in POOL_A:
                                    pe.wait_ge(ar_pool, POOL_A.index(k) + 1)
                                else:
                                    pe.wait_ge(ar_lo, DVE_A.index(k) + 2)
                            for h in range(2):
                                last = nc.tensor.matmul(ps[:, bank + h, 0:ZC], xnt[:, a, k, :], art[:, c, k, h, :],
                                                        start=(k == 0 and q == 0), stop=(k == KD - 1 and q == 2))
                if halves[-1] == 1:
                    last.then_inc(z_done, 1)

            def transpose_z(s):
                pe.wait_ge(zg_set, s + 1)
                for k in range(KB):
                    last = nc.tensor.transpose(ps[:, 4, k * P:(k + 1) * P], zg[:, k * P:(k + 1) * P], ident[:])
                last.then_inc(zt_done, 1)

            def experts_out(s, ks=range(KB), first=False):
                for q, (a, c) in enumerate(HILO):
                    if ks[0] == 0 and q == 0:
                        pe.wait_ge(zt_hi, s + 1)
                        if not first:
                            pe.wait_ge(fin_set, s)
                    if ks[0] == 0 and q == 2:
                        pe.wait_ge(zt_lo, s + 1)
                    for k in ks:
                        if first and q == 0:
                            pe.wait_ge(b_hi, k + 1)
                        if first and q == 1:
                            pe.wait_ge(b_lo, k + 1)
                        for h in range(2):
                            last = nc.tensor.matmul(ps[:, 5 + h, :], zgt[:, a, k, :],
                                                    bt[:, c, k, h * H2:(h + 1) * H2],
                                                    start=(k == 0 and q == 0), stop=(k == KB - 1 and q == 2))
                if ks[-1] == KB - 1:
                    last.then_inc(o_done, 1)

            last_g = NG - 1
            scores(last_g, range(JB - 1))
            transpose_x(0)
            scores(last_g, range(JB - 1, JB))
            pe.wait_ge(x1_done, last_g * JB)
            experts_in(0, (0,), first=True, bank=5)
            transpose_x(1, (0,))
            experts_in(0, (1,), first=True, bank=5)
            transpose_x(1, (1,))
            transpose_probs(last_g, 0)
            for s in range(1, JB + 1):
                j = s - 1
                experts_in(s, (0,))
                pe.wait_ge(xt_lo, s * 2 + 2)
                attend(last_g, j, 2)
                experts_in(s, (1,))
                if s == 1:
                    transpose_z(0)
                pe.wait_ge(x1_done, last_g * JB + j + 1)
                transpose_x(s + 1)
                experts_out(s - 1, first=(s == 1))
                if j + 1 < JB:
                    transpose_probs(last_g, j + 1)
                transpose_z(s)

            with pe.Fori(JB + 1, NT - 1) as s:
                experts_in(s)
                transpose_x(s + 1)
                experts_out(s - 1)
                transpose_z(s)
            experts_in(NT - 1)
            experts_out(NT - 2, range(KB - 1))
            transpose_z(NT - 1)
            experts_out(NT - 2, range(KB - 1, KB))
            pe.wait_ge(zt_hi, NT)
            for h in range(2):
                for q, (a, c) in enumerate(HILO):
                    if h == 0 and q == 2:
                        pe.wait_ge(zt_lo, NT)
                    for k in range(KB):
                        last = nc.tensor.matmul(ps[:, 2 + h, :], zgt_last[:, a, k, :],
                                                bt[:, c, k, h * H2:(h + 1) * H2],
                                                start=(k == 0 and q == 0), stop=(k == KB - 1 and q == 2))
                last.then_inc(last_o, 1)


def kernel(x, ctx_4096, g_xattn, g_ffn, L0_xattn_Wq, L0_xattn_bq, L0_xattn_Wk, L0_xattn_bk,
           L0_ffn_A_w, L0_ffn_B_w, L0_ffn_Wq_w, L0_ffn_keys):
    import numpy as np
    import concourse.bacc as bacc
    from concourse.bass_utils import run_bass_kernel_spmd

    B, S, D = x.shape
    x2, c2 = np.reshape(x, (B * S, D)), np.reshape(ctx_4096, (B * S, D))

    def columns(v):
        return np.reshape(v, (-1, 128)).T

    smalls = np.concatenate([columns(L0_xattn_bq), columns(L0_xattn_bk),
                             np.broadcast_to(g_xattn, (128, 1)), np.broadcast_to(g_ffn, (128, 1))], axis=1)
    arrays = {
        "x": x2, "x_t": x2.T, "ctx": c2, "ctx_t": c2.T, "smalls": smalls,
        "ident": np.eye(128, dtype=np.float32), "wq": L0_xattn_Wq, "wk": L0_xattn_Wk,
        "a_t": np.transpose(L0_ffn_A_w), "b_t": np.transpose(L0_ffn_B_w), "router_w": L0_ffn_Wq_w,
        "keys_t": np.transpose(L0_ffn_keys),
    }
    arrays = {k: np.ascontiguousarray(v) for k, v in arrays.items()}
    nc = bacc.Bacc("TRN2", target_bir_lowering=False, num_devices=1)
    args = [nc.dram_tensor(f"in_{k}", v.shape, mybir.dt.from_np(v.dtype), kind="ExternalInput").ap()
            for k, v in arrays.items()]
    out = nc.dram_tensor("out_x", (B * S, D), mybir.dt.float32, kind="ExternalOutput").ap()
    gated_xattn_moe(nc, *args, out)
    r = run_bass_kernel_spmd(nc, [{f"in_{k}": v for k, v in arrays.items()}], core_ids=[0])
    return np.reshape(r.results[0]["out_x"], (B, S, D))
```
